# Optimizing a Trainium2 kernel written in Bass

```python
import numpy as np
import jax
import jax.numpy as jnp

def _softmax(x, axis=-1):
    return jax.nn.softmax(x, axis=axis)

def _gelu(x):
    return jax.nn.gelu(x, approximate=True)

def _silu(x):
    return jax.nn.silu(x)

def _sigmoid(x):
    return jax.nn.sigmoid(x)

def _layernorm(x, axis=-1, eps=1e-05):
    m = jnp.mean(x, axis=axis, keepdims=True)
    v = jnp.var(x, axis=axis, keepdims=True)
    return (x - m) / jnp.sqrt(v + eps)

def _scatter_add(tgt, idx, src, axis=0):
    return tgt.at[idx].add(src)

def _segment_sum(src, seg, n):
    return jax.ops.segment_sum(src, seg, n)
kernel_name = 'mk_gnn_preln_d2_gnn_r32_04948d'

def setup_inputs(seed: int=0):
    np.random.seed(seed)
    _w = jnp.asarray

    def _rec_inputs():
        import jax
        import jax.numpy as jnp
        _gk = jax.random.key(seed)
        x = -0.0005121 + 1.001 * jax.random.normal(jax.random.fold_in(_gk, 1), (50000, 64), jnp.float32)
        src = jax.random.randint(jax.random.fold_in(_gk, 2), (50000,), 0, 50000, jnp.int32)
        dst = jnp.minimum((50000 * jax.random.uniform(jax.random.fold_in(_gk, 3), (50000,)) ** 2.0).astype(jnp.int32), 49999)
        _o = jnp.argsort(dst, stable=True)
        src = src[_o]
        dst = dst[_o]
        edge_type_16 = jax.random.randint(jax.random.fold_in(_gk, 12), (50000,), 0, 16, jnp.int32)
        return (x, src, dst, edge_type_16)
    x, src, dst, edge_type_16 = _rec_inputs()

    def _L0_gnn_setup():
        import jax, jax.numpy as jnp
        import numpy as np
        N_NODES = 50000
        N_EDGES = 25000
        D_IN = 64
        D_OUT = 64
        NUM_RELS = 16
        key = jax.random.key(seed)
        k1, k2, k3, k4, k5 = jax.random.split(key, 5)
        feat = jax.random.normal(k1, (N_NODES, D_IN), dtype=jnp.float32)
        weight = jax.random.normal(k2, (NUM_RELS, D_IN, D_OUT), dtype=jnp.float32) * 0.05
        src = jax.random.randint(k3, (N_EDGES,), 0, N_NODES, dtype=jnp.int32)
        dst = jax.random.randint(k4, (N_EDGES,), 0, N_NODES, dtype=jnp.int32)
        etypes = jax.random.randint(k5, (N_EDGES,), 0, NUM_RELS, dtype=jnp.int32)
        return {'feat': feat, 'weight': weight, 'src': src, 'dst': dst, 'etypes': etypes}
    _L0_gnn_all = _L0_gnn_setup()
    _L0_gnn_in = {k: v for k, v in _L0_gnn_all.items() if k in ('weight',)}
    del _L0_gnn_all

    def _L1_gnn_setup():
        import jax, jax.numpy as jnp
        import numpy as np
        N_NODES = 3125
        N_EDGES = 50000
        IN_FEAT = 64
        OUT_FEAT = 64
        NUM_RELS = 16
        NUM_BASES = 8

        def _xavier(key, shape, gain):
            fan_in, fan_out = (shape[-2], shape[-1])
            limit = gain * np.sqrt(6.0 / (fan_in + fan_out))
            return jax.random.uniform(key, shape, jnp.float32, -limit, limit)
        key = jax.random.key(seed)
        ks = jax.random.split(key, 8)
        gain = np.sqrt(2.0)
        x = jax.random.normal(ks[0], (N_NODES, IN_FEAT), jnp.float32)
        edge_src = jax.random.randint(ks[1], (N_EDGES,), 0, N_NODES)
        edge_dst = jax.random.randint(ks[2], (N_EDGES,), 0, N_NODES)
        edge_type = jax.random.randint(ks[3], (N_EDGES,), 0, NUM_RELS)
        weight = _xavier(ks[4], (NUM_BASES, IN_FEAT, OUT_FEAT), gain)
        w_comp = _xavier(ks[5], (NUM_RELS, NUM_BASES), gain)
        h_bias = jnp.zeros((OUT_FEAT,), jnp.float32)
        loop_weight = _xavier(ks[6], (IN_FEAT, OUT_FEAT), gain)
        return {'x': x, 'edge_src': edge_src, 'edge_dst': edge_dst, 'edge_type': edge_type, 'weight': weight, 'w_comp': w_comp, 'h_bias': h_bias, 'loop_weight': loop_weight}
    _L1_gnn_all = _L1_gnn_setup()
    _L1_gnn_in = {k: v for k, v in _L1_gnn_all.items() if k in ('weight', 'w_comp', 'h_bias', 'loop_weight')}
    del _L1_gnn_all
    return {'x': x, 'src': src, 'dst': dst, 'edge_type_16': edge_type_16, 'L0_gnn_weight': _L0_gnn_in['weight'], 'L1_gnn_weight': _L1_gnn_in['weight'], 'L1_gnn_w_comp': _L1_gnn_in['w_comp'], 'L1_gnn_h_bias': _L1_gnn_in['h_bias'], 'L1_gnn_loop_weight': _L1_gnn_in['loop_weight']}

def reference(x, src, dst, edge_type_16, L0_gnn_weight, L1_gnn_weight, L1_gnn_w_comp, L1_gnn_h_bias, L1_gnn_loop_weight):
    import jax
    import jax.numpy as jnp

    def _L0_gnn_ref(feat, weight, src, dst, etypes):
        import jax, jax.numpy as jnp
        import numpy as np
        N_NODES = 50000
        N_EDGES = 25000
        D_IN = 64
        D_OUT = 64
        NUM_RELS = 16
        num_rels = weight.shape[0]
        h_src = feat[src]
        msg = jnp.zeros((h_src.shape[0], weight.shape[2]), dtype=feat.dtype)
        for r in range(num_rels):
            mask = etypes == r
            msg = msg + h_src * mask[:, None].astype(feat.dtype) @ weight[r]
        out = jax.ops.segment_sum(msg, dst, num_segments=feat.shape[0])
        return out

    def _L1_gnn_ref(x, edge_src, edge_dst, edge_type, weight, w_comp, h_bias, loop_weight):
        import jax, jax.numpy as jnp
        import numpy as np
        N_NODES = 3125
        N_EDGES = 50000
        IN_FEAT = 64
        OUT_FEAT = 64
        NUM_RELS = 16
        NUM_BASES = 8

        def _xavier(key, shape, gain):
            fan_in, fan_out = (shape[-2], shape[-1])
            limit = gain * np.sqrt(6.0 / (fan_in + fan_out))
            return jax.random.uniform(key, shape, jnp.float32, -limit, limit)
        n_nodes = x.shape[0]
        W = jnp.einsum('rb,bio->rio', w_comp, weight)
        xw = jnp.einsum('ni,rio->rno', x, W)
        msg = xw[edge_type, edge_src]
        h = jax.ops.segment_sum(msg, edge_dst, num_segments=n_nodes)
        h = h + h_bias + x @ loop_weight
        return jax.nn.relu(h)
    h = jnp.maximum(_layernorm(x, axis=-1), 0.0)
    x = x + _L0_gnn_ref(h, L0_gnn_weight, src, dst, edge_type_16)
    h = jnp.maximum(_layernorm(x, axis=-1), 0.0)
    x = x + _L1_gnn_ref(h, src, dst, edge_type_16, L1_gnn_weight, L1_gnn_w_comp, L1_gnn_h_bias, L1_gnn_loop_weight)
    return x

_drawn_inputs = setup_inputs


def setup_inputs(seed=0):
    import zlib

    import numpy as np

    out = dict(_drawn_inputs(seed))
    spreads = {'L1_gnn_h_bias': (0.0, 0.1)}
    factors = {}
    for name, (base, spread) in spreads.items():
        noise = np.random.default_rng([zlib.crc32(name.encode()), seed]).standard_normal(out[name].shape)
        drawn = base * np.exp(spread * noise) if base else spread * noise
        out[name] = jnp.asarray(drawn.astype(out[name].dtype))
    for name, factor in factors.items():
        out[name] = (out[name] * factor).astype(out[name].dtype)
    return out
```

```python
from contextlib import ExitStack

import numpy as np

import concourse.bass as bass
from concourse import mybir

P = 128
D = 64
T = 4
RING = 4
A, B = 4, 4
WIN = 4
NG = 8
EPS = 1e-5

ALU = mybir.AluOpType
ACT = mybir.ActivationFunctionType
AX = mybir.AxisListType
F32 = mybir.dt.float32
BF16 = mybir.dt.bfloat16
I32 = mybir.dt.int32


def padded_tiles(n):
    return -(-n // (P * NG)) * NG


class Step:

    def __init__(self, turn, u, total, past=0):
        self.turn, self.u, self.total, self.past = turn + u // RING, u % RING, total, past
        self.fixed = isinstance(turn, int)

    def back(self, lag):
        return Step(self.turn, self.u - lag, self.total, self.past)

    @property
    def live(self):
        return not self.fixed or 0 <= RING * self.turn + self.u < self.total

    @property
    def n(self):
        return self.turn * RING + self.u

    def had(self, n):
        return not self.fixed or RING * self.turn + self.u >= n

    def count(self, each=1, ago=0):
        return (self.turn * RING + self.past * self.total + (self.u + 1 - ago)) * each

    def uses(self, each, ago=0):
        per_pass = (self.total - self.u + RING - 1) // RING
        return (self.turn + self.past * per_pass + (1 - ago)) * each


def pipeline(eng, total, lags, step, past=0):
    turns = (total - RING) // RING
    for s in range(RING):
        step(Step(0, s, total, past))
    with eng.Fori(1, 1 + turns) as turn:
        for u in range(RING):
            step(Step(turn, u, total, past))
    for s in range(RING * (1 + turns), total + lags):
        step(Step(s // RING, s % RING, total, past))


def two_layer_rgcn(nc, x, src_q, dst_rows, dst_cols, type_rows, type_cols, W0, V1, comp1, bias1, loop1, out):
    N = x.shape[0]
    R = W0.shape[0]
    NB = V1.shape[0]
    NT = padded_tiles(N)
    NF = N // P
    NR = N - NF * P
    ET = dst_cols.shape[1]
    QUADS = ET // T
    GROUPS = NT // NG
    TPP = dst_rows.shape[1] // P
    EP = type_rows.shape[1]
    WC = WIN * D
    LAST = (NT - 1) * D
    assert R == A * B and A == 4 and ET % T == 0 and D * 2 == P

    with ExitStack() as ctx:
        def sb(name, shape, dt=F32):
            return ctx.enter_context(nc.sbuf_tensor(name, shape, dt))

        def psum(name, shape):
            return ctx.enter_context(nc.psum_tensor(name, shape, F32))

        def sem(name):
            return ctx.enter_context(nc.semaphore(name))

        mask_dram = nc.dram_tensor("mask_dram", [A, ET * P], BF16).ap()
        span_dram = nc.dram_tensor("span_dram", [2, ET], I32).ap()
        x1_dram = nc.dram_tensor("x1_dram", [NT * P, D], F32).ap()
        h1_dram = nc.dram_tensor("h1_dram", [NT * P, D], F32).ap()

        acc = sb("acc", [P, (NT + WIN - 1) * D])
        iota = sb("iota", [P, WIN * P])
        row_i = sb("row_i", [P, 1], I32)
        row = sb("row", [P, 1])
        ident = sb("ident", [P, P])
        eps = sb("eps", [P, 1])
        dst_i = sb("dst_i", [P, ET], I32)
        low_i = sb("low_i", [P, ET], I32)
        low_f = sb("low_f", [P, ET])
        rel0 = sb("rel0", [P, ET])
        rel = sb("rel", [P, ET])
        drow = sb("drow", [ET // TPP, TPP, P], I32)
        lohi = sb("lohi", [ET // TPP, 2, TPP], I32)
        span = sb("span", [P, 2, ET], I32)
        wide = sb("wide", [P, ET], I32)
        widest = sb("widest", [P, 1], I32)
        passes = sb("passes", [P, 1], I32)
        off0 = sb("off0", [P, ET], I32)
        off = sb("off", [P, ET], I32)
        type_r = sb("type_r", [P, EP], I32)
        type_a = sb("type_a", [P, EP], I32)
        mask_r = sb("mask_r", [P, A, EP], BF16)
        type_c = sb("type_c", [P, ET], I32)
        type_b = sb("type_b", [P, ET], I32)
        is_b = sb("is_b", [P, ET, B])
        w0 = sb("w0", [P, 2, B, D])
        w1 = sb("w1", [P, 2 * B, D])
        wt = sb("wt", [P, 2 * B, D])
        v1 = sb("v1", [P, NB, D])
        comp = sb("comp", [P, 2 * B, NB])
        loopw = sb("loopw", [P, D])
        bias = sb("bias", [P, D])
        idx = sb("idx", [P, RING, T], I32)
        mask = sb("mask", [P, RING, 2, T * P], BF16)
        rows = sb("rows", [P, RING, T, D])
        stats = sb("stats", [P, 2, NG, 6])
        mv = sb("mv", [P, 2, NG, 2])
        std = sb("std", [P, 2, NG])
        rstd = sb("rstd", [P, 2, NG])
        pick = sb("pick", [P, 2, T, B])
        twice = sb("twice", [P, 2, T, 2, D])
        masked = sb("masked", [P, 2, 2, T * P])
        picked = sb("picked", [P, 2, T, B, D])
        half = sb("half", [P, 2, T, 2, D])
        msg = sb("msg", [P, 2, T, D])
        hot = sb("hot", [P, 2, T, WIN * P])
        iota_i = hot[:, 0, 0].bitcast(I32)
        dense = sb("dense", [P, RING, NG * D])
        hT_sb = masked[:, 0]

        ps_t = [psum(f"ps_t{i}", [P, T * P]) for i in range(2)]
        ps_y = [[psum(f"ps_y{i}{j}", [P, 2, B, D]) for j in range(2)] for i in range(2)]
        ps_w = [psum(f"ps_w{i}", [P, 2, WC]) for i in range(2)]

        const_in = sem("const_in")
        edges_in = sem("edges_in")
        acc_in = sem("acc_in")
        made = sem("made")
        c_dve = sem("c_dve")
        span_out = sem("span_out")
        span_in = sem("span_in")
        mask_out = sem("mask_out")
        ready = sem("ready")

        class Layer:

            def __init__(s, n):
                s.idx_in = [sem(f"idx_in{n}{i}") for i in range(RING)]
                s.mask_in = [sem(f"mask_in{n}{i}") for i in range(RING)]
                s.rows_in = [sem(f"rows_in{n}{i}") for i in range(RING)]
                s.stats_done = sem(f"stats_done{n}")
                s.mv_done = sem(f"mv_done{n}")
                s.std_done = sem(f"std_done{n}")
                s.rstd_done = sem(f"rstd_done{n}")
                s.pick_done = sem(f"pick_done{n}")
                s.twice_done = sem(f"twice_done{n}")
                s.turned = sem(f"turned{n}")
                s.masked_done = sem(f"masked_done{n}")
                s.prod_done = sem(f"prod_done{n}")
                s.picked_done = sem(f"picked_done{n}")
                s.half_done = sem(f"half_done{n}")
                s.msg_done = sem(f"msg_done{n}")
                s.hot_done = sem(f"hot_done{n}")
                s.win_done = sem(f"win_done{n}")
                s.added = sem(f"added{n}")
                s.start = sem(f"start{n}")
                s.moved = sem(f"moved{n}")

        layers = [Layer(0), Layer(1)]
        held = {name: sem(f"held_{name}") for name in ("pool", "sp", "dve")}

        x1_done = sem("x1_done")
        m_stats = sem("m_stats")
        m_mv = sem("m_mv")
        m_std = sem("m_std")
        m_rstd = sem("m_rstd")
        m_cent = sem("m_cent")
        m_h = sem("m_h")
        m_x1_out = [sem(f"m_x1_out{i}") for i in range(RING)]
        m_h_out = [sem(f"m_h_out{i}") for i in range(RING)]
        m_turned = sem("m_turned")
        m_hT = sem("m_hT")
        m_loop = sem("m_loop")
        m_acc = sem("m_acc")
        f_x1_in = [sem(f"f_x1_in{i}") for i in range(RING)]
        f_sum = sem("f_sum")
        f_out = [sem(f"f_out{i}") for i in range(RING)]

        acc_tiles = acc[:].rearrange("p (t d) -> p t d", d=D)
        acc_pairs = acc[:, 0:NT * D].rearrange("p (t odd d) -> p odd t d", odd=2, d=D)
        LAGS = 3

        def load_passes(eng, kind):
            return nc.values_load(passes[0:1, 0:1], engines=[kind], min_val=1, max_val=-(-NT // WIN),
                                  skip_runtime_bounds_check_because="a span of node tiles over WIN")

        def group_dram(table, n):
            return table[bass.ds(n * (NG * P), NG * P), :].rearrange("(t p) d -> p t d", p=P)

        def pass_start(eng, L, k):
            eng.wait_ge(L.start, k + 1)

        block = ctx.enter_context(nc.Block())

        @block.sync
        def _(sp):
            sp.dma_start(drow[:], dst_rows.rearrange("q (t e) -> q t e", e=P)).then_inc(edges_in, 16)
            sp.dma_start(type_r[:], type_rows).then_inc(edges_in, 16)
            sp.dma_start(dst_i[:], dst_cols).then_inc(edges_in, 16)
            sp.dma_start(type_c[:], type_cols).then_inc(edges_in, 16)
            w_split = W0.rearrange("(p a b) d o -> a d p b o", p=2, a=2)
            v_split = V1.rearrange("c d o -> d c o")
            comp_split = comp1.rearrange("(p a b) c -> a p b c", p=2, a=2)
            for a2 in range(2):
                half_p = slice(a2 * D, a2 * D + D)
                for p in range(2):
                    sp.dma_start(w0[half_p, p], w_split[a2, :, p]).then_inc(const_in, 16)
                    sp.dma_start(comp[half_p, p * B:p * B + B],
                                 comp_split[a2, p].unsqueeze(0).broadcast_to([D, B, NB])).then_inc(const_in, 16)
                sp.dma_start(v1[half_p], v_split).then_inc(const_in, 16)
                sp.dma_start(loopw[half_p], loop1).then_inc(const_in, 16)
            sp.dma_start(bias[:], bias1.unsqueeze(0).broadcast_to([P, D])).then_inc(const_in, 16)
            sp.wait_ge(c_dve, 4)
            sp.dma_start(span_dram.rearrange("h (q t) -> q h t", t=TPP), lohi[:]).then_inc(span_out, 16)
            sp.wait_ge(span_out, 16)
            sp.dma_start(span[0:1], span_dram.unsqueeze(0)).then_inc(span_in, 16)
            sp.dma_start(low_i[:], span_dram[0].unsqueeze(0).broadcast_to([P, ET])).then_inc(span_in, 16)
            sp.wait_ge(c_dve, 9)
            sp.dma_start(mask_dram.rearrange("a (q e) -> q a e", e=EP), mask_r[:]).then_inc(mask_out, 16)
            sp.wait_ge(mask_out, 16)

            def edge_loads(L):
                passes_r = load_passes(sp, mybir.EngineType.SP)

                def step(s):
                    if not s.live:
                        return
                    if s.had(RING):
                        sp.wait_ge(L.rows_in[s.u], s.uses(16 * T, ago=1))
                        sp.sem_inc(held["sp"], 1)
                    sp.dma_start(idx[:, s.u], src_q[bass.ds(s.n, 1)].rearrange("q p t -> (q p) t")).then_inc(L.idx_in[s.u], 16)
                    if s.had(RING):
                        sp.wait_ge(L.masked_done, s.count(ago=RING))
                        sp.sem_inc(held["sp"], 1)
                    for p in range(2):
                        for a2 in range(2):
                            sp.dma_start(
                                mask[a2 * D:a2 * D + D, s.u, p],
                                mask_dram[2 * p + a2, bass.ds(s.n * (T * P), T * P)].unsqueeze(0)
                                .broadcast_to([D, T * P])).then_inc(L.mask_in[s.u], 16)

                with sp.Fori(0, passes_r) as k:
                    pass_start(sp, L, k)
                    pipeline(sp, QUADS, 0, step, k)

            sp.wait_ge(ready, 1)
            edge_loads(layers[0])

            def mid(s):
                if s.live:
                    if s.fixed and s.n == 0:
                        sp.wait_ge(x1_done, 1)
                    sp.dma_start(group_dram(x1_dram, s.n), acc_tiles[:, bass.ds(s.n * NG, NG)]).then_inc(m_x1_out[s.u], 16)
                    sp.wait_ge(m_h, s.count())
                    sp.sem_inc(held["sp"], 1)
                    sp.dma_start(group_dram(h1_dram, s.n),
                                 dense[:, s.u].rearrange("p (t d) -> p t d", d=D)).then_inc(m_h_out[s.u], 16)

            pipeline(sp, GROUPS, 0, mid)
            for u in range(RING):
                sp.wait_ge(m_x1_out[u], 16 * ((GROUPS - u + RING - 1) // RING))
                sp.wait_ge(m_h_out[u], 16 * ((GROUPS - u + RING - 1) // RING))
            edge_loads(layers[1])

            def last(s):
                if s.live:
                    if s.had(RING):
                        sp.wait_ge(f_out[s.u], s.uses(16, ago=1))
                        sp.sem_inc(held["sp"], 1)
                    sp.dma_start(dense[:, s.u].rearrange("p (t d) -> p t d", d=D),
                                 group_dram(x1_dram, s.n)).then_inc(f_x1_in[s.u], 16)
                w = s.back(2)
                if w.live:
                    sp.wait_ge(f_sum, w.count())
                    sp.sem_inc(held["sp"], 1)
                    whole = not w.fixed or (w.n + 1) * NG <= NF
                    shown = dense[:, w.u].rearrange("p (t d) -> p t d", d=D)
                    if whole:
                        sp.dma_start(group_dram(out, w.n), shown).then_inc(f_out[w.u], 16)
                    else:
                        t0 = NF - w.n * NG
                        if t0:
                            sp.dma_start(out[w.n * NG * P:NF * P, :].rearrange("(t p) d -> p t d", p=P),
                                         shown[:, 0:t0]).then_inc(f_out[w.u], 16)
                        if NR:
                            sp.dma_start(out[NF * P:N, :], shown[0:NR, t0]).then_inc(f_out[w.u], 16)

            pipeline(sp, GROUPS, 2, last)
            ends = [16 * ((GROUPS - u + RING - 1) // RING) for u in range(RING)]
            ends[(GROUPS - 1) % RING] += 16 * ((NF > (GROUPS - 1) * NG) + (NR > 0) - 1)
            for u in range(RING):
                sp.wait_ge(f_out[u], ends[u])

        @block.gpsimd
        def _(pool):
            nc.gpsimd.iota(iota_i, pattern=[[1, WIN * P]], base=0, channel_multiplier=0).then_inc(made, 1)
            nc.gpsimd.iota(row_i[:], pattern=[[0, 1]], base=0, channel_multiplier=1).then_inc(made, 1)
            nc.gpsimd.memset(eps[:], EPS).then_inc(made, 1)
            nc.gpsimd.memset(acc[:, NF * D:], 0.0).then_inc(made, 1)
            def gathers(L, table, layer):
                passes_r = load_passes(pool, mybir.EngineType.Pool)

                def step(s):
                    if not s.live:
                        return
                    pool.wait_ge(L.idx_in[s.u], s.uses(16))
                    if s.had(RING):
                        pool.wait_ge(L.twice_done, s.count(ago=RING))
                    pool.sem_inc(held["pool"], 1)
                    for t in range(T):
                        nc.gpsimd.indirect_dma_start(
                            out=rows[:, s.u, t], out_offset=None, in_=table,
                            in_offset=bass.IndirectOffsetOnAxis(ap=idx[:, s.u, t:t + 1], axis=0),
                        ).then_inc(L.rows_in[s.u], 16)

                with pool.Fori(0, passes_r) as k:
                    pass_start(pool, L, k)
                    pipeline(pool, QUADS, 0, step, k)

            pool.wait_ge(ready, 1)
            gathers(layers[0], x, 0)
            for u in range(RING):
                pool.wait_ge(m_h_out[u], 16 * ((GROUPS - u + RING - 1) // RING))
            gathers(layers[1], h1_dram, 1)

        @block.tensor
        def _(pe):
            def edge_products(L, weights, layer):
                passes_r = load_passes(pe, mybir.EngineType.PE)

                def turn_rows(s):
                    pe.wait_ge(L.twice_done, s.count())
                    if s.had(2):
                        pe.wait_ge(L.masked_done, s.count(ago=2))
                    for t in range(T):
                        mm = pe.transpose(ps_t[s.u % 2][:, t * P:t * P + P],
                                          twice[:, s.u % 2, t].rearrange("e a d -> e (a d)"), ident[:])
                    mm.then_inc(L.turned, 1)

                def products(s):
                    pe.wait_ge(L.masked_done, s.count())
                    for h in range(2):
                        if s.had(2):
                            pe.wait_ge(L.picked_done, s.count(each=2, ago=2) - (1 - h))
                        for j in range(2):
                            t = 2 * h + j
                            for p in range(2):
                                mm = pe.matmul(ps_y[s.u % 2][h][:, j].rearrange("e b o -> e (b o)"),
                                               masked[:, s.u % 2, p, t * P:t * P + P],
                                               weights(p), start=(p == 0), stop=(p == 1))
                        mm.then_inc(L.prod_done, 1)

                def windows(s):
                    pe.wait_ge(L.hot_done, s.count())
                    pe.wait_ge(L.msg_done, s.count())
                    for h in range(2):
                        if s.had(1):
                            pe.wait_ge(L.added, s.count(each=T, ago=1) - (2 - 2 * h))
                        for j in range(2):
                            t = 2 * h + j
                            for w in range(WIN):
                                mm = pe.matmul(ps_w[h][:, j, w * D:w * D + D],
                                               hot[:, s.u % 2, t, w * P:w * P + P],
                                               msg[:, s.u % 2, t], start=True, stop=True)
                        mm.then_inc(L.win_done, 1)

                def step(s):
                    if s.live:
                        turn_rows(s)
                    if s.back(1).live:
                        products(s.back(1))
                    if s.back(2).live:
                        windows(s.back(2))

                with pe.Fori(0, passes_r) as k:
                    pass_start(pe, L, k)
                    pipeline(pe, QUADS, LAGS, step, k)

            pe.wait_ge(ready, 1)
            pe.wait_ge(const_in, 16 * 13)
            edge_products(layers[0], lambda p: w0[:, p].rearrange("k b o -> k (b o)"), 0)

            def mid(s):
                if s.live:
                    pe.wait_ge(m_h, s.count())
                    if s.had(1):
                        pe.wait_ge(m_hT, s.count(ago=1))
                    for j in range(NG // 2):
                        mm = pe.transpose(ps_t[0][:, j * P:j * P + P], dense[:, s.u, j * P:j * P + P], ident[:])
                    mm.then_inc(m_turned, 1)
                b = s.back(1)
                if b.live:
                    pe.wait_ge(m_hT, b.count())
                    if b.had(2):
                        pe.wait_ge(m_acc, b.count(ago=2))
                    for g in range(NG):
                        of = slice(g % 2 * D, g % 2 * D + D)
                        mm = pe.matmul(ps_y[b.u % 2][g % 2][:, 0, g // 2],
                                       hT_sb[of, b.u % 2, g // 2 * P:g // 2 * P + P], loopw[of],
                                       start=True, stop=True)
                    mm.then_inc(m_loop, 1)

            pipeline(pe, GROUPS, 1, mid)
            edge_products(layers[1], lambda p: w1[:, p * B:p * B + B].rearrange("k b o -> k (b o)"), 1)

        @block.scalar
        def _(act):
            act.wait_ge(made, 4)
            act.dma_start(acc_tiles[:, 0:NF], x[0:NF * P, :].rearrange("(t p) d -> p t d", p=P)).then_inc(acc_in, 16)
            if NR:
                act.dma_start(acc_tiles[0:NR, NF], x[NF * P:N, :]).then_inc(acc_in, 16)

            def edge_picks(L, layer):
                passes_r = load_passes(act, mybir.EngineType.Activation)

                def deviation(s):
                    act.wait_ge(L.mv_done, s.count())
                    if s.had(2):
                        act.wait_ge(L.rstd_done, s.count(ago=2))
                    act.activation(std[:, s.u % 2, 0:T], mv[:, s.u % 2, 0:T, 1], ACT.Sqrt,
                                   bias=eps[:]).then_inc(L.std_done, 1)

                def picks(s):
                    if layer == 0:
                        act.wait_ge(L.pick_done, s.count())
                    if s.had(2):
                        act.wait_ge(L.half_done, s.count(ago=2))
                    for h in range(2):
                        act.wait_ge(L.prod_done, s.count(each=2) - (1 - h))
                        for j in range(2):
                            t = 2 * h + j
                            for b in range(B):
                                by = (pick[:, s.u % 2, t, b:b + 1] if layer == 0 else
                                      is_b[:, bass.ds(s.n * T + t, 1), b])
                                a = act.activation(picked[:, s.u % 2, t, b], ps_y[s.u % 2][h][:, j, b],
                                                   ACT.Copy, scale=by)
                        a.then_inc(L.picked_done, 1)

                def double(s):
                    act.wait_ge(L.rows_in[s.u], s.uses(16 * T))
                    if s.had(2):
                        act.wait_ge(L.turned, s.count(ago=2))
                    act.activation(twice[:, s.u % 2], rows[:, s.u].unsqueeze(2).broadcast_to([P, T, 2, D]),
                                   ACT.Copy).then_inc(L.twice_done, 1)

                def step(s):
                    if s.live:
                        if layer == 0:
                            deviation(s)
                        else:
                            double(s)
                    if s.back(1).live:
                        picks(s.back(1))

                with act.Fori(0, passes_r) as k:
                    pass_start(act, L, k)
                    pipeline(act, QUADS, LAGS, step, k)

            act.wait_ge(ready, 1)
            edge_picks(layers[0], 0)

            def mid(s):
                if s.live:
                    act.wait_ge(m_mv, s.count())
                    if s.had(2):
                        act.wait_ge(m_rstd, s.count(ago=2))
                    act.activation(std[:, s.u % 2], mv[:, s.u % 2, :, 1], ACT.Sqrt, bias=eps[:]).then_inc(m_std, 1)
                b = s.back(1)
                if b.live:
                    act.wait_ge(m_rstd, b.count())
                    act.wait_ge(m_cent, b.count())
                    for g in range(NG):
                        a = act.activation(dense[:, b.u, g * D:g * D + D], dense[:, b.u, g * D:g * D + D],
                                           ACT.Relu, scale=rstd[:, b.u % 2, g:g + 1])
                    a.then_inc(m_h, 1)
                c = s.back(2)
                if c.live:
                    if c.had(2):
                        act.wait_ge(m_loop, c.count(ago=2))
                    act.wait_ge(m_turned, c.count())
                    act.activation(hT_sb[:, c.u % 2], ps_t[0][:], ACT.Copy).then_inc(m_hT, 1)

            pipeline(act, GROUPS, 2, mid)
            edge_picks(layers[1], 1)

        @block.vector
        def _(dve):
            steps = [0]

            def done(ins):
                steps[0] += 1
                ins.then_inc(c_dve, 1)
                dve.wait_ge(c_dve, steps[0])

            dve.wait_ge(edges_in, 16 * 4)
            done(dve.tensor_reduce(lohi[:, 0], drow[:], AX.X, ALU.min))
            done(dve.tensor_scalar(lohi[:, 0], lohi[:, 0], P.bit_length() - 1, None, ALU.arith_shift_right))
            done(dve.tensor_reduce(lohi[:, 1], drow[:], AX.X, ALU.max))
            done(dve.tensor_scalar(lohi[:, 1], lohi[:, 1], P.bit_length() - 1, None, ALU.arith_shift_right))
            done(dve.tensor_scalar(type_a[:], type_r[:], B.bit_length() - 1, None, ALU.arith_shift_right))
            for a in range(A):
                done(dve.tensor_scalar(mask_r[:, a], type_a[:], float(a), None, ALU.is_equal))
            done(dve.tensor_scalar(type_b[:], type_c[:], B - 1, None, ALU.bitwise_and))
            for b in range(B):
                done(dve.tensor_scalar(is_b[:, :, b], type_b[:], float(b), None, ALU.is_equal))
            dve.wait_ge(made, 4)
            done(dve.tensor_copy(iota[:], iota_i))
            done(dve.tensor_copy(row[:], row_i[:]))
            done(dve.tensor_scalar(ident[:], iota[:, 0:P], row[:, 0:1], None, ALU.is_equal))
            dve.wait_ge(span_in, 32)
            done(dve.tensor_copy(low_f[:], low_i[:]))
            done(dve.tensor_copy(rel[:], dst_i[:]))
            done(dve.scalar_tensor_tensor(rel0[:], low_f[:], float(-P), rel[:], ALU.mult, ALU.add))
            done(dve.tensor_scalar(off0[0:1], span[0:1, 0], D, None, ALU.mult))
            done(dve.tensor_tensor(wide[0:1], span[0:1, 1], span[0:1, 0], ALU.subtract))
            done(dve.tensor_reduce(widest[0:1], wide[0:1], AX.X, ALU.max))
            done(dve.tensor_scalar(widest[0:1], widest[0:1], WIN.bit_length() - 1, None, ALU.arith_shift_right))
            done(dve.tensor_scalar(passes[0:1], widest[0:1], 1, None, ALU.add))
            dve.wait_ge(const_in, 16 * 13)
            for c in range(NB):
                to = w1 if c == 0 else wt
                done(dve.tensor_tensor(to[:], v1[:, c].unsqueeze(1).broadcast_to([P, 2 * B, D]),
                                       comp[:, :, c:c + 1].broadcast_to([P, 2 * B, D]), ALU.mult))
                if c:
                    done(dve.tensor_tensor(w1[:], w1[:], wt[:], ALU.add))
            dve.tensor_copy(rel[:], rel0[:]).then_inc(c_dve, 1)
            dve.tensor_copy(off[0:1], off0[0:1]).then_inc(c_dve, 1)
            steps[0] += 2
            dve.wait_ge(c_dve, steps[0])
            dve.nop().then_inc(ready, 1)

            def edge_sums(L, layer):
                passes_r = load_passes(dve, mybir.EngineType.DVE)

                def normalise(s):
                    dve.wait_ge(L.rows_in[s.u], s.uses(16 * T))
                    i = s.u % 2
                    for t in range(T):
                        b = dve.bn_stats(stats[:, i, t], rows[:, s.u, t])
                    b.then_inc(L.stats_done, 1)
                    dve.wait_ge(L.stats_done, s.count())
                    dve.sem_inc(held["dve"], 1)
                    for t in range(T):
                        b = dve.bn_aggr(mv[:, i, t], stats[:, i, t])
                    b.then_inc(L.mv_done, 1)
                    dve.wait_ge(L.mv_done, s.count())
                    if s.had(2):
                        dve.wait_ge(L.turned, s.count(ago=2))
                    dve.tensor_tensor(twice[:, i], rows[:, s.u].unsqueeze(2).broadcast_to([P, T, 2, D]),
                                      mv[:, i, 0:T, 0:1].unsqueeze(3).broadcast_to([P, T, 2, D]), ALU.subtract).then_inc(L.twice_done, 1)

                def invert(s):
                    i = s.u % 2
                    dve.wait_ge(L.std_done, s.count())
                    if s.had(2):
                        dve.wait_ge(L.picked_done, s.count(each=2, ago=2))
                    dve.reciprocal(rstd[:, i, 0:T], std[:, i, 0:T]).then_inc(L.rstd_done, 1)
                    dve.wait_ge(L.rstd_done, s.count())
                    dve.tensor_tensor(pick[:, i], is_b[:, bass.ds(s.n * T, T)],
                                      rstd[:, i, 0:T].unsqueeze(2).broadcast_to([P, T, B]),
                                      ALU.mult).then_inc(L.pick_done, 1)

                def mask_rows(s):
                    i = s.u % 2
                    dve.wait_ge(L.turned, s.count())
                    dve.wait_ge(L.mask_in[s.u], s.uses(16 * 4))
                    if s.had(2):
                        dve.wait_ge(L.prod_done, s.count(each=2, ago=2))
                    for p in range(2):
                        m = dve.scalar_tensor_tensor(masked[:, i, p], ps_t[i][:], 0.0, mask[:, s.u, p],
                                                     ALU.max, ALU.mult)
                    m.then_inc(L.masked_done, 1)

                def one_hot(s, t):
                    i = s.u % 2
                    if t == 0:
                        if s.had(2):
                            dve.wait_ge(L.win_done, s.count(each=2, ago=2))
                    h = dve.tensor_scalar(hot[:, i, t], iota[:], rel[:, bass.ds(s.n * T + t, 1)], None,
                                          ALU.is_equal)
                    if t == T - 1:
                        h.then_inc(L.hot_done, 1)

                def sum_first(s):
                    i = s.u % 2
                    dve.wait_ge(L.picked_done, s.count(each=2))
                    dve.tensor_tensor(half[:, i], picked[:, i, :, 0:2], picked[:, i, :, 2:4],
                                      ALU.add).then_inc(L.half_done, 1)

                def sum_second(s):
                    i = s.u % 2
                    dve.wait_ge(L.half_done, s.count())
                    if s.had(2):
                        dve.wait_ge(L.win_done, s.count(each=2, ago=2))
                    dve.tensor_tensor(msg[:, i], half[:, i, :, 0], half[:, i, :, 1], ALU.add).then_inc(L.msg_done, 1)

                def add_window(s, t, at):
                    if t % 2 == 0:
                        dve.wait_ge(L.win_done, s.count(each=2) - (1 - t // 2))
                    if s.had(1) or t > 0:
                        dve.wait_ge(L.added, s.count(each=T) - (T - t))
                    to = acc[:, bass.ds(at, WC)]
                    dve.tensor_tensor(to, ps_w[t // 2][:, t % 2], to, ALU.add).then_inc(L.added, 1)

                def step(s):
                    a, o, m, c = s.back(3), s.back(1), s.back(1), s.back(2)
                    at = []
                    if a.live:
                        at = nc.values_load_multi_w_load_instructions(
                            off[0:1, bass.ds(a.n * T, T)], engines=[mybir.EngineType.DVE], min_val=0, max_val=LAST,
                            skip_runtime_bounds_check_because="the windows are held to acc where they are set")[1]
                    if layer == 0 and s.live:
                        normalise(s)
                    if m.live:
                        mask_rows(m)
                    if c.live:
                        sum_first(c)
                    for t in range(T):
                        if a.live:
                            add_window(a, t, at[t])
                        if o.live:
                            one_hot(o, t)
                        if t == 0 and c.live:
                            sum_second(c)
                        if t == 1 and layer == 0 and s.live:
                            invert(s)

                with dve.Fori(0, passes_r) as k:
                    dve.nop().then_inc(L.start, 1)
                    pipeline(dve, QUADS, LAGS, step, k)
                    dve.wait_ge(L.added, (k + 1) * (QUADS * T))
                    dve.tensor_scalar(rel[:], rel[:], float(-WIN * P), None, ALU.add).then_inc(L.moved, 1)
                    dve.tensor_scalar(off[0:1], off[0:1], WC, LAST, ALU.add, ALU.min).then_inc(L.moved, 1)
                    dve.wait_ge(L.moved, (k + 1) * 2)

            dve.wait_ge(acc_in, 16 * (1 + (NR > 0)))
            edge_sums(layers[0], 0)
            dve.nop().then_inc(x1_done, 1)

            def mid(s):
                i = s.u % 2
                if s.live:
                    one = acc_tiles[:, bass.ds(s.n * NG, NG)]
                    for g in range(NG):
                        b = dve.bn_stats(stats[:, i, g], acc_tiles[:, bass.ds(s.n * NG + g, 1)].rearrange("p o d -> p (o d)"))
                    b.then_inc(m_stats, 1)
                    dve.wait_ge(m_stats, s.count())
                    dve.sem_inc(held["dve"], 1)
                    for g in range(NG):
                        b = dve.bn_aggr(mv[:, i, g], stats[:, i, g])
                    b.then_inc(m_mv, 1)
                    dve.wait_ge(m_mv, s.count())
                    if s.had(RING):
                        dve.wait_ge(m_h_out[s.u], s.uses(16, ago=1))
                        dve.wait_ge(m_turned, s.count(ago=RING))
                    dve.tensor_tensor(dense[:, s.u].rearrange("p (t d) -> p t d", d=D), one,
                                      mv[:, i, :, 0:1].broadcast_to([P, NG, D]), ALU.subtract).then_inc(m_cent, 1)
                    dve.wait_ge(m_std, s.count())
                    if s.had(2):
                        dve.wait_ge(m_h, s.count(ago=2))
                    dve.reciprocal(rstd[:, i], std[:, i]).then_inc(m_rstd, 1)
                b = s.back(3)
                if b.live:
                    dve.wait_ge(m_loop, b.count())
                    dve.wait_ge(m_x1_out[b.u], b.uses(16))
                    for odd in range(2):
                        a = dve.tensor_tensor(acc_pairs[:, odd, bass.ds(b.n * (NG // 2), NG // 2)],
                                              ps_y[b.u % 2][odd][:, 0],
                                              bias[:].unsqueeze(1).broadcast_to([P, NG // 2, D]), ALU.add)
                    a.then_inc(m_acc, 1)

            pipeline(dve, GROUPS, 3, mid)
            dve.wait_ge(m_acc, GROUPS)
            dve.tensor_copy(rel[:], rel0[:]).then_inc(ready, 1)
            dve.tensor_copy(off[0:1], off0[0:1]).then_inc(ready, 1)
            dve.wait_ge(ready, 3)
            edge_sums(layers[1], 1)

            def last(s):
                if s.live:
                    dve.wait_ge(f_x1_in[s.u], s.uses(16))
                    shown = dense[:, s.u]
                    dve.scalar_tensor_tensor(shown, acc[:, bass.ds(s.n * (NG * D), NG * D)], 0.0, shown,
                                             ALU.max, ALU.add).then_inc(f_sum, 1)

            pipeline(dve, GROUPS, 0, last)


_OUTS = [((50000, 64), "float32")]


def kernel(x, src, dst, edge_type_16, L0_gnn_weight, L1_gnn_weight, L1_gnn_w_comp, L1_gnn_h_bias, L1_gnn_loop_weight):
    import concourse.bacc as bacc
    from concourse.bass_utils import run_bass_kernel_spmd

    x = np.asarray(x)
    src, dst, kind = (np.asarray(v).astype(np.int32) for v in (src, dst, edge_type_16))
    n, e, rels = x.shape[0], src.shape[0], np.asarray(L0_gnn_weight).shape[0]
    tiles = padded_tiles(e)
    filled = [np.concatenate([v, np.full(tiles * P - e, c, np.int32)])
              for v, c in ((src, 0), (dst, n - 1), (kind, rels))]
    src_q = np.ascontiguousarray(filled[0].reshape(tiles // T, T, P).transpose(0, 2, 1))
    cols = [np.ascontiguousarray(v.reshape(tiles, P).T) for v in filled[1:]]
    arrays = {
        "x": x, "src_q": src_q, "dst_rows": filled[1].reshape(-1, T * P), "dst_cols": cols[0],
        "type_rows": filled[2].reshape(P, -1), "type_cols": cols[1],
        "W0": L0_gnn_weight, "V1": L1_gnn_weight, "comp1": L1_gnn_w_comp, "bias1": L1_gnn_h_bias,
        "loop1": L1_gnn_loop_weight,
    }
    arrays = {f"in_{k}": np.ascontiguousarray(v) for k, v in arrays.items()}
    nc = bacc.Bacc("TRN2", target_bir_lowering=False, num_devices=1)
    args = [nc.dram_tensor(k, v.shape, mybir.dt.from_np(v.dtype), kind="ExternalInput").ap() for k, v in arrays.items()]
    args += [nc.dram_tensor(f"out_{i}", s, mybir.dt.from_np(np.dtype(d)), kind="ExternalOutput").ap()
             for i, (s, d) in enumerate(_OUTS)]
    two_layer_rgcn(nc, *args)
    r = run_bass_kernel_spmd(nc, [arrays], core_ids=[0])
    return r.results[0]["out_0"]
```

```python
from contextlib import ExitStack

import numpy as np

import concourse.bass as bass
from concourse import mybir

P = 128
D = 64
T = 4
RING = 4
A, B = 4, 4
WIN = 4
NG = 8
EPS = 1e-5

ALU = mybir.AluOpType
ACT = mybir.ActivationFunctionType
AX = mybir.AxisListType
F32 = mybir.dt.float32
BF16 = mybir.dt.bfloat16
I32 = mybir.dt.int32
I16 = mybir.dt.int16


def padded_tiles(n):
    return -(-n // (P * NG)) * NG


class Step:

    def __init__(self, turn, u, total, past=0):
        self.turn, self.u, self.total, self.past = turn + u // RING, u % RING, total, past
        self.fixed = isinstance(turn, int)

    def back(self, lag):
        return Step(self.turn, self.u - lag, self.total, self.past)

    @property
    def live(self):
        return not self.fixed or 0 <= RING * self.turn + self.u < self.total

    @property
    def n(self):
        return self.turn * RING + self.u

    def had(self, n):
        return not self.fixed or RING * self.turn + self.u >= n

    def count(self, each=1, ago=0):
        return (self.turn * RING + self.past * self.total + (self.u + 1 - ago)) * each

    def uses(self, each, ago=0):
        per_pass = (self.total - self.u + RING - 1) // RING
        return (self.turn + self.past * per_pass + (1 - ago)) * each


def pipeline(eng, total, lags, step, past=0, head=1):
    turns = total // RING - head
    for s in range(RING * head):
        step(Step(s // RING, s % RING, total, past))
    with eng.Fori(head, head + turns) as turn:
        for u in range(RING):
            step(Step(turn, u, total, past))
    for s in range(RING * (head + turns), total + lags):
        step(Step(s // RING, s % RING, total, past))


def two_layer_rgcn(nc, x, src_q, dst_rows, dst_cols, type_rows, type_cols, W0, V1, comp1, bias1, loop1, out):
    N = x.shape[0]
    R = W0.shape[0]
    NB = V1.shape[0]
    NT = padded_tiles(N)
    NF = N // P
    NR = N - NF * P
    ET = dst_cols.shape[1]
    QUADS = ET // T
    GROUPS = NT // NG
    TPP = dst_rows.shape[1] // P
    EP = type_rows.shape[1]
    WC = WIN * D
    LAST = (NT - 1) * D
    assert R == A * B and A == 4 and ET % T == 0 and D * 2 == P
    assert QUADS * T == NT and NF // T == QUADS - 1 and NF % T and NR

    with ExitStack() as ctx:
        def sb(name, shape, dt=F32):
            return ctx.enter_context(nc.sbuf_tensor(name, shape, dt))

        def psum(name, shape):
            return ctx.enter_context(nc.psum_tensor(name, shape, F32))

        def sem(name):
            return ctx.enter_context(nc.semaphore(name))

        mask_dram = nc.dram_tensor("mask_dram", [A, ET * P], BF16).ap()
        span_dram = nc.dram_tensor("span_dram", [2, ET], I32).ap()
        x1_dram = nc.dram_tensor("x1_dram", [P, NT * D], F32).ap()
        h1_dram = nc.dram_tensor("h1_dram", [NT * P, D], F32).ap()

        acc = sb("acc", [P, (NT + WIN - 1) * D])
        iota = sb("iota", [P, WIN * P], I16)
        row_i = sb("row_i", [P, 1], I32)
        row = sb("row", [P, 1])
        ident = sb("ident", [P, P])
        eps = sb("eps", [P, 1])
        dst_i = sb("dst_i", [P, ET], I32)
        low_i = sb("low_i", [P, ET], I32)
        low_f = sb("low_f", [P, ET])
        rel0 = sb("rel0", [P, ET])
        rel = sb("rel", [P, ET])
        drow = sb("drow", [ET // TPP, TPP, P], I32)
        lohi = sb("lohi", [ET // TPP, 2, TPP], I32)
        span = sb("span", [P, 2, ET], I32)
        wide = sb("wide", [P, ET], I32)
        widest = sb("widest", [P, 1], I32)
        passes = sb("passes", [P, 1], I32)
        off0 = sb("off0", [1, QUADS, T], I32)
        off = sb("off", [1, QUADS, T], I32)
        type_r = sb("type_r", [P, EP], I32)
        type_a = sb("type_a", [P, EP], I32)
        mask_r = sb("mask_r", [P, A, EP], BF16)
        type_c = sb("type_c", [P, ET], I32)
        type_b = sb("type_b", [P, ET], I32)
        is_b = sb("is_b", [P, ET, B])
        w0 = sb("w0", [P, 2, B, D])
        w1 = sb("w1", [P, 2 * B, D])
        wt = sb("wt", [P, 2 * B, D])
        v1 = sb("v1", [P, NB, D])
        comp = sb("comp", [P, 2 * B, NB])
        loopw = sb("loopw", [P, D])
        bias = sb("bias", [P, D])
        idx = sb("idx", [P, RING, T], I32)
        mask = sb("mask", [P, RING, 2, T * P], BF16)
        rows = sb("rows", [P, RING, T, D])
        x_part = sb("x_part", [P, RING, T, D])
        first_pass = sb("first_pass", [P, 1])
        stats = sb("stats", [P, 2, NG, 6])
        mv = sb("mv", [P, 2, NG, 2])
        std = sb("std", [P, 2, NG])
        rstd = sb("rstd", [P, 2, NG])
        pick = sb("pick", [P, 2, T, B])
        twice = sb("twice", [P, 2, T, 2, D])
        masked = sb("masked", [P, 2, 2, T * P])
        picked = sb("picked", [P, 2, T, B, D])
        half = sb("half", [P, 2, T, 2, D])
        msg = sb("msg", [P, 2, T, D])
        rest = sb("rest", [P, 2, T, D])
        low = sb("low", [P, 2, T, D], BF16)
        hot = sb("hot", [P, 2, T, WIN * P], BF16)
        negm = sb("negm", [P, 2, T])
        iota_i = hot[:, 0, 0:2].rearrange("p t w -> p (t w)").bitcast(I32)
        dense = sb("dense", [P, RING, NG * D])
        hT_sb = masked[:, 0]

        ps_t = [psum(f"ps_t{i}", [P, T * P]) for i in range(2)]
        ps_y = [[psum(f"ps_y{i}{j}", [P, 2, B, D]) for j in range(2)] for i in range(2)]
        ps_w = [psum(f"ps_w{i}", [P, 2, WC]) for i in range(2)]

        const_in = sem("const_in")
        edges_in = sem("edges_in")
        acc_zero = sem("acc_zero")
        made = sem("made")
        c_dve = sem("c_dve")
        span_out = sem("span_out")
        span_in = sem("span_in")
        mask_out = sem("mask_out")
        ready = sem("ready")

        class Layer:

            def __init__(s, n):
                s.idx_in = [sem(f"idx_in{n}{i}") for i in range(RING)]
                s.mask_in = [sem(f"mask_in{n}{i}") for i in range(RING)]
                s.rows_in = [sem(f"rows_in{n}{i}") for i in range(RING)]
                s.stats_done = sem(f"stats_done{n}")
                s.mv_done = sem(f"mv_done{n}")
                s.std_done = sem(f"std_done{n}")
                s.rstd_done = sem(f"rstd_done{n}")
                s.pick_done = sem(f"pick_done{n}")
                s.twice_done = sem(f"twice_done{n}")
                s.turned = sem(f"turned{n}")
                s.masked_done = sem(f"masked_done{n}")
                s.prod_done = sem(f"prod_done{n}")
                s.picked_done = sem(f"picked_done{n}")
                s.negm_done = sem(f"negm_done{n}")
                s.half_done = sem(f"half_done{n}")
                s.rest_done = sem(f"rest_done{n}")
                s.low_done = sem(f"low_done{n}")
                s.msg_done = sem(f"msg_done{n}")
                s.hot_done = sem(f"hot_done{n}")
                s.win_done = sem(f"win_done{n}")
                s.added = sem(f"added{n}")
                s.x_in = [sem(f"x_in{n}{i}") for i in range(RING)]
                s.x_tail = sem(f"x_tail{n}")
                s.x_added = sem(f"x_added{n}")
                s.start = sem(f"start{n}")
                s.moved = sem(f"moved{n}")

        layers = [Layer(0), Layer(1)]
        held = {name: sem(f"held_{name}") for name in ("pool", "sp", "dve")}

        x1_done = sem("x1_done")
        m_stats = sem("m_stats")
        m_mv = sem("m_mv")
        m_std = sem("m_std")
        m_rstd = sem("m_rstd")
        m_cent = sem("m_cent")
        m_scaled = sem("m_scaled")
        m_h = sem("m_h")
        m_x1_out = [sem(f"m_x1_out{i}") for i in range(RING)]
        m_h_out = [sem(f"m_h_out{i}") for i in range(RING)]
        m_turned = sem("m_turned")
        m_hT = sem("m_hT")
        m_loop = sem("m_loop")
        m_acc = sem("m_acc")
        f_x1_in = [sem(f"f_x1_in{i}") for i in range(RING)]
        f_bias = sem("f_bias")
        f_sum = sem("f_sum")
        f_out = [sem(f"f_out{i}") for i in range(RING)]

        acc_tiles = acc[:].rearrange("p (t d) -> p t d", d=D)
        acc_pairs = acc[:, 0:NT * D].rearrange("p (t odd d) -> p odd t d", odd=2, d=D)
        LAGS = 3
        WON = 3
        HALVES_AFTER = 5

        def dense_tiles(s):
            return dense[:, s.u].rearrange("p (t d) -> p t d", d=D)


        def load_passes(eng, kind):
            return nc.values_load(passes[0:1, 0:1], engines=[kind], min_val=1, max_val=-(-NT // WIN),
                                  skip_runtime_bounds_check_because="a span of node tiles over WIN")

        def high(words):
            return words.bitcast(BF16).rearrange("... (d two) -> ... d two", two=2)[..., 1]

        def group_dram(table, n):
            return table[bass.ds(n * (NG * P), NG * P), :].rearrange("(t p) d -> p t d", p=P)

        def pass_start(eng, L, k):
            eng.wait_ge(L.start, k + 1)

        block = ctx.enter_context(nc.Block())

        @block.sync
        def _(sp):
            sp.dma_start(drow[:], dst_rows.rearrange("q (t e) -> q t e", e=P)).then_inc(edges_in, 16)
            sp.dma_start(type_r[:], type_rows).then_inc(edges_in, 16)
            sp.dma_start(dst_i[:], dst_cols).then_inc(edges_in, 16)
            sp.dma_start(type_c[:], type_cols).then_inc(edges_in, 16)
            w_split = W0.rearrange("(p a b) d o -> a d p b o", p=2, a=2)
            v_split = V1.rearrange("c d o -> d c o")
            comp_split = comp1.rearrange("(p a b) c -> a p b c", p=2, a=2)
            for a2 in range(2):
                half_p = slice(a2 * D, a2 * D + D)
                for p in range(2):
                    sp.dma_start(w0[half_p, p], w_split[a2, :, p]).then_inc(const_in, 16)
                    sp.dma_start(comp[half_p, p * B:p * B + B],
                                 comp_split[a2, p].unsqueeze(0).broadcast_to([D, B, NB])).then_inc(const_in, 16)
                sp.dma_start(v1[half_p], v_split).then_inc(const_in, 16)
                sp.dma_start(loopw[half_p], loop1).then_inc(const_in, 16)
            sp.dma_start(bias[:], bias1.unsqueeze(0).broadcast_to([P, D])).then_inc(const_in, 16)
            sp.wait_ge(c_dve, 4)
            sp.dma_start(span_dram.rearrange("h (q t) -> q h t", t=TPP), lohi[:]).then_inc(span_out, 16)
            sp.wait_ge(span_out, 16)
            sp.dma_start(span[0:1], span_dram.unsqueeze(0)).then_inc(span_in, 16)
            sp.dma_start(low_i[:], span_dram[0].unsqueeze(0).broadcast_to([P, ET])).then_inc(span_in, 16)
            sp.wait_ge(c_dve, 9)
            sp.dma_start(mask_dram.rearrange("a (q e) -> q a e", e=EP), mask_r[:]).then_inc(mask_out, 16)
            sp.wait_ge(mask_out, 16)

            def x_load(L, s):
                if not s.fixed or s.n < NF // T:
                    sp.dma_start(x_part[:, s.u],
                                 x[bass.ds(s.n * (T * P), T * P), :].rearrange("(t p) d -> p t d", p=P)).then_inc(L.x_in[s.u], 16)
                else:
                    sp.dma_start(x_part[:, s.u, 0:NF % T],
                                 x[s.n * T * P:NF * P, :].rearrange("(t p) d -> p t d", p=P)).then_inc(L.x_in[s.u], 16)
                    sp.dma_start(x_part[0:NR, s.u, NF % T], x[NF * P:N, :]).then_inc(L.x_tail, 16)

            def edge_loads(L, layer):
                passes_r = load_passes(sp, mybir.EngineType.SP)

                def step(s):
                    if not s.live:
                        return
                    if s.had(RING):
                        sp.wait_ge(L.rows_in[s.u], s.uses(16 * T, ago=1))
                        sp.sem_inc(held["sp"], 1)
                    sp.dma_start(idx[:, s.u], src_q[bass.ds(s.n, 1)].rearrange("q p t -> (q p) t")).then_inc(L.idx_in[s.u], 16)
                    if s.had(RING):
                        sp.wait_ge(L.masked_done, s.count(ago=RING))
                        sp.sem_inc(held["sp"], 1)
                    for p in range(2):
                        for a2 in range(2):
                            sp.dma_start(
                                mask[a2 * D:a2 * D + D, s.u, p],
                                mask_dram[2 * p + a2, bass.ds(s.n * (T * P), T * P)].unsqueeze(0)
                                .broadcast_to([D, T * P])).then_inc(L.mask_in[s.u], 16)
                    if layer == 0:
                        if s.had(RING):
                            sp.wait_ge(L.x_added, s.count(ago=RING))
                            sp.sem_inc(held["sp"], 1)
                        x_load(L, s)

                with sp.Fori(0, passes_r) as k:
                    pass_start(sp, L, k)
                    pipeline(sp, QUADS, 0, step, k)

            sp.wait_ge(ready, 1)
            edge_loads(layers[0], 0)

            def mid(s):
                if s.live:
                    if s.fixed and s.n == 0:
                        sp.wait_ge(x1_done, 1)
                    columns = bass.ds(s.n * (NG * D), NG * D)
                    sp.dma_start(x1_dram[:, columns], acc[:, columns]).then_inc(m_x1_out[s.u], 16)
                    sp.wait_ge(m_h, s.count())
                    sp.sem_inc(held["sp"], 1)
                    sp.dma_start(group_dram(h1_dram, s.n),
                                 dense[:, s.u].rearrange("p (t d) -> p t d", d=D)).then_inc(m_h_out[s.u], 16)

            pipeline(sp, GROUPS, 0, mid)
            edge_loads(layers[1], 1)
            for u in range(RING):
                sp.wait_ge(m_x1_out[u], 16 * ((GROUPS - u + RING - 1) // RING))
                sp.wait_ge(m_h_out[u], 16 * ((GROUPS - u + RING - 1) // RING))

            def last(s):
                if s.live:
                    if s.had(RING):
                        sp.wait_ge(f_out[s.u], s.uses(16, ago=1))
                        sp.sem_inc(held["sp"], 1)
                    sp.dma_start(dense[:, s.u], x1_dram[:, bass.ds(s.n * (NG * D), NG * D)]).then_inc(f_x1_in[s.u], 16)
                w = s.back(2)
                if w.live:
                    sp.wait_ge(f_sum, w.count())
                    sp.sem_inc(held["sp"], 1)
                    whole = not w.fixed or (w.n + 1) * NG <= NF
                    shown = dense[:, w.u].rearrange("p (t d) -> p t d", d=D)
                    if whole:
                        sp.dma_start(group_dram(out, w.n), shown).then_inc(f_out[w.u], 16)
                    else:
                        t0 = NF - w.n * NG
                        if t0:
                            sp.dma_start(out[w.n * NG * P:NF * P, :].rearrange("(t p) d -> p t d", p=P),
                                         shown[:, 0:t0]).then_inc(f_out[w.u], 16)
                        if NR:
                            sp.dma_start(out[NF * P:N, :], shown[0:NR, t0]).then_inc(f_out[w.u], 16)

            pipeline(sp, GROUPS, 2, last)
            ends = [16 * ((GROUPS - u + RING - 1) // RING) for u in range(RING)]
            ends[(GROUPS - 1) % RING] += 16 * ((NF > (GROUPS - 1) * NG) + (NR > 0) - 1)
            for u in range(RING):
                sp.wait_ge(f_out[u], ends[u])

        @block.gpsimd
        def _(pool):
            nc.gpsimd.iota(iota_i, pattern=[[1, WIN * P]], base=0, channel_multiplier=0).then_inc(made, 1)
            nc.gpsimd.iota(row_i[:], pattern=[[0, 1]], base=0, channel_multiplier=1).then_inc(made, 1)
            nc.gpsimd.memset(eps[:], EPS).then_inc(made, 1)
            nc.gpsimd.memset(first_pass[:], 1.0).then_inc(made, 1)
            nc.gpsimd.memset(acc[:], 0.0).then_inc(acc_zero, 1)
            def gathers(L, table):
                passes_r = load_passes(pool, mybir.EngineType.Pool)

                def halve(s):
                    i = s.u % 2
                    pool.wait_ge(L.picked_done, s.count(each=2))
                    if s.had(2):
                        pool.wait_ge(L.msg_done, s.count(ago=2))
                    nc.gpsimd.tensor_tensor(half[:, i], picked[:, i, :, 0:2], picked[:, i, :, 2:4],
                                            ALU.add).then_inc(L.half_done, 1)

                def step(s):
                    if s.back(HALVES_AFTER).live:
                        halve(s.back(HALVES_AFTER))
                    if s.live:
                        gather(s)

                def gather(s):
                    pool.wait_ge(L.idx_in[s.u], s.uses(16))
                    if s.had(RING):
                        pool.wait_ge(L.twice_done, s.count(ago=RING))
                    pool.sem_inc(held["pool"], 1)
                    for t in range(T):
                        nc.gpsimd.indirect_dma_start(
                            out=rows[:, s.u, t], out_offset=None, in_=table,
                            in_offset=bass.IndirectOffsetOnAxis(ap=idx[:, s.u, t:t + 1], axis=0),
                        ).then_inc(L.rows_in[s.u], 16)

                with pool.Fori(0, passes_r) as k:
                    pass_start(pool, L, k)
                    pipeline(pool, QUADS, HALVES_AFTER, step, k, head=2)

            pool.wait_ge(ready, 1)
            gathers(layers[0], x)

            def mid(s):
                i = s.u % 2
                if s.live:
                    if s.had(RING):
                        pool.wait_ge(m_h_out[s.u], s.uses(16, ago=1))
                        pool.wait_ge(m_turned, s.count(ago=RING))
                    pool.wait_ge(m_mv, s.count())
                    nc.gpsimd.tensor_tensor(dense_tiles(s), acc_tiles[:, bass.ds(s.n * NG, NG)],
                                            mv[:, i, :, 0:1].broadcast_to([P, NG, D]),
                                            ALU.subtract).then_inc(m_cent, 1)
                b = s.back(1)
                if b.live:
                    pool.wait_ge(m_cent, b.count())
                    pool.wait_ge(m_rstd, b.count())
                    nc.gpsimd.tensor_tensor(dense_tiles(b), dense_tiles(b),
                                            rstd[:, b.u % 2].unsqueeze(2).broadcast_to([P, NG, D]),
                                            ALU.mult).then_inc(m_scaled, 1)

            pipeline(pool, GROUPS, 1, mid)
            for u in range(RING):
                pool.wait_ge(m_h_out[u], 16 * ((GROUPS - u + RING - 1) // RING))
            gathers(layers[1], h1_dram)

        @block.tensor
        def _(pe):
            def edge_products(L, weights, layer):
                passes_r = load_passes(pe, mybir.EngineType.PE)

                def turn_rows(s):
                    pe.wait_ge(L.twice_done, s.count())
                    if s.had(2):
                        pe.wait_ge(L.masked_done, s.count(ago=2))
                    for t in range(T):
                        mm = pe.transpose(ps_t[s.u % 2][:, t * P:t * P + P],
                                          twice[:, s.u % 2, t].rearrange("e a d -> e (a d)"), ident[:])
                    mm.then_inc(L.turned, 1)

                def products(s):
                    pe.wait_ge(L.masked_done, s.count())
                    for h in range(2):
                        if s.had(2):
                            pe.wait_ge(L.picked_done, s.count(each=2, ago=2) - (1 - h))
                        for j in range(2):
                            t = 2 * h + j
                            for p in range(2):
                                mm = pe.matmul(ps_y[s.u % 2][h][:, j].rearrange("e b o -> e (b o)"),
                                               masked[:, s.u % 2, p, t * P:t * P + P],
                                               weights(p), start=(p == 0), stop=(p == 1))
                        mm.then_inc(L.prod_done, 1)

                def windows(s):
                    pe.wait_ge(L.hot_done, s.count())
                    pe.wait_ge(L.low_done, s.count())
                    for h in range(2):
                        if s.had(1):
                            pe.wait_ge(L.added, s.count(each=T, ago=1) - (2 - 2 * h))
                        for j in range(2):
                            t = 2 * h + j
                            parts = high(msg[:, s.u % 2, t]), high(rest[:, s.u % 2, t]), low[:, s.u % 2, t]
                            for w in range(WIN):
                                for n, part in enumerate(parts):
                                    mm = pe.matmul(ps_w[h][:, j, w * D:w * D + D],
                                                   hot[:, s.u % 2, t, w * P:w * P + P],
                                                   part, start=(n == 0), stop=(n == 2))
                        mm.then_inc(L.win_done, 1)

                def step(s):
                    if s.back(1).live:
                        products(s.back(1))
                    if s.live:
                        turn_rows(s)
                    if s.back(2).live:
                        windows(s.back(2))

                with pe.Fori(0, passes_r) as k:
                    pass_start(pe, L, k)
                    pipeline(pe, QUADS, LAGS, step, k)

            pe.wait_ge(ready, 1)
            pe.wait_ge(const_in, 16 * 13)
            edge_products(layers[0], lambda p: w0[:, p].rearrange("k b o -> k (b o)"), 0)

            def mid(s):
                if s.live:
                    pe.wait_ge(m_h, s.count())
                    if s.had(1):
                        pe.wait_ge(m_hT, s.count(ago=1))
                    for j in range(NG // 2):
                        mm = pe.transpose(ps_t[0][:, j * P:j * P + P], dense[:, s.u, j * P:j * P + P], ident[:])
                    mm.then_inc(m_turned, 1)
                b = s.back(1)
                if b.live:
                    pe.wait_ge(m_hT, b.count())
                    if b.had(2):
                        pe.wait_ge(m_acc, b.count(ago=2))
                    for g in range(NG):
                        of = slice(g % 2 * D, g % 2 * D + D)
                        mm = pe.matmul(ps_y[b.u % 2][g % 2][:, 0, g // 2],
                                       hT_sb[of, b.u % 2, g // 2 * P:g // 2 * P + P], loopw[of],
                                       start=True, stop=True)
                    mm.then_inc(m_loop, 1)

            pipeline(pe, GROUPS, 1, mid)
            edge_products(layers[1], lambda p: w1[:, p * B:p * B + B].rearrange("k b o -> k (b o)"), 1)

        @block.scalar
        def _(act):
            def edge_picks(L, layer):
                passes_r = load_passes(act, mybir.EngineType.Activation)

                def deviation(s):
                    act.wait_ge(L.mv_done, s.count())
                    if s.had(2):
                        act.wait_ge(L.rstd_done, s.count(ago=2))
                    act.activation(std[:, s.u % 2, 0:T], mv[:, s.u % 2, 0:T, 1], ACT.Sqrt,
                                   bias=eps[:]).then_inc(L.std_done, 1)

                def picks(s):
                    if layer == 0:
                        act.wait_ge(L.pick_done, s.count())
                    if s.had(2):
                        act.wait_ge(L.half_done, s.count(ago=2))
                    for h in range(2):
                        act.wait_ge(L.prod_done, s.count(each=2) - (1 - h))
                        for j in range(2):
                            t = 2 * h + j
                            for b in range(B):
                                by = (pick[:, s.u % 2, t, b:b + 1] if layer == 0 else
                                      is_b[:, bass.ds(s.n * T + t, 1), b])
                                a = act.activation(picked[:, s.u % 2, t, b], ps_y[s.u % 2][h][:, j, b],
                                                   ACT.Copy, scale=by)
                        a.then_inc(L.picked_done, 1)

                def double(s):
                    act.wait_ge(L.rows_in[s.u], s.uses(16 * T))
                    if s.had(2):
                        act.wait_ge(L.turned, s.count(ago=2))
                    act.activation(twice[:, s.u % 2], rows[:, s.u].unsqueeze(2).broadcast_to([P, T, 2, D]),
                                   ACT.Copy).then_inc(L.twice_done, 1)

                def centre(s):
                    act.wait_ge(L.negm_done, s.count())
                    if s.had(2):
                        act.wait_ge(L.turned, s.count(ago=2))
                    for t in range(T):
                        a = act.activation(twice[:, s.u % 2, t],
                                           rows[:, s.u, t].unsqueeze(1).broadcast_to([P, 2, D]),
                                           ACT.Relu, bias=negm[:, s.u % 2, t:t + 1])
                    a.then_inc(L.twice_done, 1)

                def step(s):
                    if s.live:
                        if layer == 0:
                            centre(s)
                            deviation(s)
                        else:
                            double(s)
                    if s.back(1).live:
                        picks(s.back(1))

                with act.Fori(0, passes_r) as k:
                    pass_start(act, L, k)
                    pipeline(act, QUADS, LAGS, step, k)

            act.wait_ge(ready, 1)
            edge_picks(layers[0], 0)

            def mid(s):
                if s.live:
                    act.wait_ge(m_mv, s.count())
                    if s.had(2):
                        act.wait_ge(m_rstd, s.count(ago=2))
                    act.activation(std[:, s.u % 2], mv[:, s.u % 2, :, 1], ACT.Sqrt, bias=eps[:]).then_inc(m_std, 1)
                b = s.back(1)
                if b.live:
                    act.wait_ge(m_scaled, b.count())
                    act.activation(dense[:, b.u], dense[:, b.u], ACT.Relu).then_inc(m_h, 1)
                c = s.back(2)
                if c.live:
                    if c.had(2):
                        act.wait_ge(m_loop, c.count(ago=2))
                    act.wait_ge(m_turned, c.count())
                    act.activation(hT_sb[:, c.u % 2], ps_t[0][:], ACT.Copy).then_inc(m_hT, 1)
                e = s.back(3)
                if e.live:
                    act.wait_ge(m_loop, e.count())
                    act.wait_ge(m_x1_out[e.u], e.uses(16))
                    for odd in range(2):
                        a = act.activation(acc_pairs[:, odd, bass.ds(e.n * (NG // 2), NG // 2)],
                                           ps_y[e.u % 2][odd][:, 0], ACT.Copy)
                    a.then_inc(m_acc, 1)

            pipeline(act, GROUPS, 3, mid)
            edge_picks(layers[1], 1)

        @block.vector
        def _(dve):
            steps = [0]

            def done(ins):
                steps[0] += 1
                ins.then_inc(c_dve, 1)
                dve.wait_ge(c_dve, steps[0])

            dve.wait_ge(edges_in, 16 * 4)
            done(dve.tensor_reduce(lohi[:, 0], drow[:], AX.X, ALU.min))
            done(dve.tensor_scalar(lohi[:, 0], lohi[:, 0], P.bit_length() - 1, None, ALU.arith_shift_right))
            done(dve.tensor_reduce(lohi[:, 1], drow[:], AX.X, ALU.max))
            done(dve.tensor_scalar(lohi[:, 1], lohi[:, 1], P.bit_length() - 1, None, ALU.arith_shift_right))
            done(dve.tensor_scalar(type_a[:], type_r[:], B.bit_length() - 1, None, ALU.arith_shift_right))
            for a in range(A):
                done(dve.tensor_scalar(mask_r[:, a], type_a[:], float(a), None, ALU.is_equal))
            done(dve.tensor_scalar(type_b[:], type_c[:], B - 1, None, ALU.bitwise_and))
            for b in range(B):
                done(dve.tensor_scalar(is_b[:, :, b], type_b[:], float(b), None, ALU.is_equal))
            dve.wait_ge(made, 4)
            done(dve.tensor_copy(iota[:], iota_i))
            done(dve.tensor_copy(row[:], row_i[:]))
            done(dve.tensor_scalar(ident[:], iota[:, 0:P], row[:, 0:1], None, ALU.is_equal))
            dve.wait_ge(span_in, 32)
            done(dve.tensor_copy(low_f[:], low_i[:]))
            done(dve.tensor_copy(rel[:], dst_i[:]))
            done(dve.scalar_tensor_tensor(rel0[:], low_f[:], float(-P), rel[:], ALU.mult, ALU.add))
            by_quad = span[0:1, 0].rearrange("p (q t) -> p q t", t=T)
            done(dve.tensor_scalar(off0[:], by_quad, D, None, ALU.mult))
            done(dve.tensor_tensor(wide[0:1], span[0:1, 1], span[0:1, 0], ALU.subtract))
            done(dve.tensor_reduce(widest[0:1], wide[0:1], AX.X, ALU.max))
            done(dve.tensor_scalar(widest[0:1], widest[0:1], WIN.bit_length() - 1, None, ALU.arith_shift_right))
            done(dve.tensor_scalar(passes[0:1], widest[0:1], 1, None, ALU.add))
            dve.wait_ge(const_in, 16 * 13)
            for c in range(NB):
                to = w1 if c == 0 else wt
                done(dve.tensor_tensor(to[:], v1[:, c].unsqueeze(1).broadcast_to([P, 2 * B, D]),
                                       comp[:, :, c:c + 1].broadcast_to([P, 2 * B, D]), ALU.mult))
                if c:
                    done(dve.tensor_tensor(w1[:], w1[:], wt[:], ALU.add))
            dve.tensor_copy(rel[:], rel0[:]).then_inc(c_dve, 1)
            dve.tensor_copy(off[:], off0[:]).then_inc(c_dve, 1)
            steps[0] += 2
            dve.wait_ge(c_dve, steps[0])
            dve.nop().then_inc(ready, 1)

            def edge_sums(L, layer):
                passes_r = load_passes(dve, mybir.EngineType.DVE)

                def statistics(s):
                    dve.wait_ge(L.rows_in[s.u], s.uses(16 * T))
                    for t in range(T):
                        b = dve.bn_stats(stats[:, s.u % 2, t], rows[:, s.u, t])
                    b.then_inc(L.stats_done, 1)

                def means(s):
                    i = s.u % 2
                    dve.wait_ge(L.stats_done, s.count())
                    dve.sem_inc(held["dve"], 1)
                    for t in range(T):
                        b = dve.bn_aggr(mv[:, i, t], stats[:, i, t])
                    b.then_inc(L.mv_done, 1)

                def negate(s):
                    i = s.u % 2
                    dve.wait_ge(L.mv_done, s.count())
                    dve.tensor_scalar(negm[:, i], mv[:, i, 0:T, 0], -1.0, None, ALU.mult).then_inc(L.negm_done, 1)

                def invert(s):
                    i = s.u % 2
                    dve.wait_ge(L.std_done, s.count())
                    dve.reciprocal(rstd[:, i, 0:T], std[:, i, 0:T]).then_inc(L.rstd_done, 1)

                def deviate(s):
                    i = s.u % 2
                    dve.wait_ge(L.rstd_done, s.count())
                    if s.had(2):
                        dve.wait_ge(L.picked_done, s.count(each=2, ago=2))
                    dve.tensor_tensor(pick[:, i], is_b[:, bass.ds(s.n * T, T)],
                                      rstd[:, i, 0:T].unsqueeze(2).broadcast_to([P, T, B]),
                                      ALU.mult).then_inc(L.pick_done, 1)

                def mask_rows(s):
                    i = s.u % 2
                    dve.wait_ge(L.turned, s.count())
                    dve.wait_ge(L.mask_in[s.u], s.uses(16 * 4))
                    if s.had(2):
                        dve.wait_ge(L.prod_done, s.count(each=2, ago=2))
                    for p in range(2):
                        m = dve.tensor_tensor(masked[:, i, p], ps_t[i][:], mask[:, s.u, p], ALU.mult)
                    m.then_inc(L.masked_done, 1)

                def one_hot(s, t):
                    i = s.u % 2
                    if t == 0:
                        if s.had(2):
                            dve.wait_ge(L.win_done, s.count(each=2, ago=2))
                    h = dve.tensor_scalar(hot[:, i, t], iota[:], rel[:, bass.ds(s.n * T + t, 1)], None,
                                          ALU.is_equal)
                    if t == T - 1:
                        h.then_inc(L.hot_done, 1)

                def sum_up(s):
                    i = s.u % 2
                    dve.wait_ge(L.half_done, s.count())
                    if s.had(2):
                        dve.wait_ge(L.win_done, s.count(each=2, ago=2))
                    dve.tensor_tensor(msg[:, i], half[:, i, :, 0], half[:, i, :, 1], ALU.add).then_inc(L.msg_done, 1)

                def split_rest(s):
                    i = s.u % 2
                    dve.wait_ge(L.msg_done, s.count())
                    dve.tensor_tensor(rest[:, i], msg[:, i], high(msg[:, i]), ALU.subtract).then_inc(L.rest_done, 1)

                def split_low(s):
                    i = s.u % 2
                    dve.wait_ge(L.rest_done, s.count())
                    dve.tensor_tensor(low[:, i], rest[:, i], high(rest[:, i]), ALU.subtract).then_inc(L.low_done, 1)

                def add_x(s):
                    dve.wait_ge(L.x_in[s.u], s.uses(16))
                    if s.fixed and s.n == NF // T:
                        dve.wait_ge(L.x_tail, (s.past + 1) * 16)
                    if s.back(WON).live:
                        dve.wait_ge(L.added, s.back(WON).count(each=T))
                    if s.had(1):
                        dve.wait_ge(L.x_added, s.count(ago=1))
                    to = acc[:, bass.ds(s.n * (T * D), T * D)]
                    dve.scalar_tensor_tensor(to, x_part[:, s.u].rearrange("p t d -> p (t d)"), first_pass[:, 0:1],
                                             to, ALU.mult, ALU.add).then_inc(L.x_added, 1)

                def add_window(s, t, at):
                    if t % 2 == 0:
                        dve.wait_ge(L.win_done, s.count(each=2) - (1 - t // 2))
                    before = s.back(1 - WON)
                    if layer == 0 and t == 0 and before.live:
                        dve.wait_ge(L.x_added, before.count())
                    if s.had(1) or t > 0:
                        dve.wait_ge(L.added, s.count(each=T) - (T - t))
                    to = acc[:, bass.ds(at, WC)]
                    dve.tensor_tensor(to, ps_w[t // 2][:, t % 2], to, ALU.add).then_inc(L.added, 1)

                def step(s):
                    new, turned, summed, won = s, s.back(1), s.back(2), s.back(WON)
                    ln = layer == 0 and new.live
                    if won.live:
                        at = nc.values_load_multi_w_load_instructions(
                            off[:, bass.ds(won.n, 1)].rearrange("p q t -> p (q t)"), engines=[mybir.EngineType.DVE],
                            min_val=0, max_val=LAST,
                            skip_runtime_bounds_check_because="the windows are held to acc where they are set")[1]

                    def tile(t):
                        if won.live:
                            add_window(won, t, at[t])
                        if turned.live:
                            one_hot(turned, t)

                    if ln:
                        statistics(new)
                    if turned.live:
                        mask_rows(turned)
                    if ln:
                        means(new)
                    tile(0)
                    if ln:
                        negate(new)
                    if summed.live:
                        sum_up(summed)
                    tile(1)
                    if summed.live:
                        split_rest(summed)
                    tile(2)
                    if ln:
                        invert(new)
                    if summed.live:
                        split_low(summed)
                    if ln:
                        deviate(new)
                    tile(3)
                    if ln:
                        add_x(new)

                with dve.Fori(0, passes_r) as k:
                    dve.nop().then_inc(L.start, 1)
                    pipeline(dve, QUADS, LAGS, step, k)
                    dve.wait_ge(L.added, (k + 1) * (QUADS * T))
                    if layer == 0:
                        dve.wait_ge(L.x_added, (k + 1) * QUADS)
                        dve.memset(first_pass[:], 0.0).then_inc(L.moved, 1)
                    dve.tensor_scalar(rel[:], rel[:], float(-WIN * P), None, ALU.add).then_inc(L.moved, 1)
                    dve.tensor_scalar(off[:], off[:], WC, LAST, ALU.add, ALU.min).then_inc(L.moved, 1)
                    dve.wait_ge(L.moved, (k + 1) * (3 if layer == 0 else 2))

            dve.wait_ge(acc_zero, 1)
            edge_sums(layers[0], 0)
            dve.nop().then_inc(x1_done, 1)

            def mid(s):
                i = s.u % 2
                if s.live:
                    for g in range(NG):
                        b = dve.bn_stats(stats[:, i, g], acc_tiles[:, bass.ds(s.n * NG + g, 1)].rearrange("p o d -> p (o d)"))
                    b.then_inc(m_stats, 1)
                    if s.had(2):
                        dve.wait_ge(m_cent, s.count(ago=2))
                    dve.wait_ge(m_stats, s.count())
                    dve.sem_inc(held["dve"], 1)
                    for g in range(NG):
                        b = dve.bn_aggr(mv[:, i, g], stats[:, i, g])
                    b.then_inc(m_mv, 1)
                b = s.back(1)
                if b.live:
                    dve.wait_ge(m_std, b.count())
                    if b.had(2):
                        dve.wait_ge(m_scaled, b.count(ago=2))
                    dve.reciprocal(rstd[:, b.u % 2], std[:, b.u % 2]).then_inc(m_rstd, 1)

            pipeline(dve, GROUPS, 1, mid)
            dve.wait_ge(m_acc, GROUPS)
            dve.tensor_copy(rel[:], rel0[:]).then_inc(ready, 1)
            dve.tensor_copy(off[:], off0[:]).then_inc(ready, 1)
            dve.wait_ge(ready, 3)
            edge_sums(layers[1], 1)

            def last(s):
                if s.live:
                    part = acc_tiles[:, bass.ds(s.n * NG, NG)]
                    dve.tensor_tensor(part, part, bias[:].unsqueeze(1).broadcast_to([P, NG, D]),
                                      ALU.add).then_inc(f_bias, 1)
                b = s.back(1)
                if b.live:
                    dve.wait_ge(f_bias, b.count())
                    dve.wait_ge(f_x1_in[b.u], b.uses(16))
                    shown = dense[:, b.u]
                    dve.scalar_tensor_tensor(shown, acc[:, bass.ds(b.n * (NG * D), NG * D)], 0.0, shown,
                                             ALU.max, ALU.add).then_inc(f_sum, 1)

            pipeline(dve, GROUPS, 1, last)


_OUTS = [((50000, 64), "float32")]


def kernel(x, src, dst, edge_type_16, L0_gnn_weight, L1_gnn_weight, L1_gnn_w_comp, L1_gnn_h_bias, L1_gnn_loop_weight):
    import concourse.bacc as bacc
    from concourse.bass_utils import run_bass_kernel_spmd

    x = np.asarray(x)
    src, dst, kind = (np.asarray(v).astype(np.int32) for v in (src, dst, edge_type_16))
    n, e, rels = x.shape[0], src.shape[0], np.asarray(L0_gnn_weight).shape[0]
    tiles = padded_tiles(e)
    filled = [np.concatenate([v, np.full(tiles * P - e, c, np.int32)])
              for v, c in ((src, 0), (dst, n - 1), (kind, rels))]
    src_q = np.ascontiguousarray(filled[0].reshape(tiles // T, T, P).transpose(0, 2, 1))
    cols = [np.ascontiguousarray(v.reshape(tiles, P).T) for v in filled[1:]]
    arrays = {
        "x": x, "src_q": src_q, "dst_rows": filled[1].reshape(-1, T * P), "dst_cols": cols[0],
        "type_rows": filled[2].reshape(P, -1), "type_cols": cols[1],
        "W0": L0_gnn_weight, "V1": L1_gnn_weight, "comp1": L1_gnn_w_comp, "bias1": L1_gnn_h_bias,
        "loop1": L1_gnn_loop_weight,
    }
    arrays = {f"in_{k}": np.ascontiguousarray(v) for k, v in arrays.items()}
    nc = bacc.Bacc("TRN2", target_bir_lowering=False, num_devices=1)
    args = [nc.dram_tensor(k, v.shape, mybir.dt.from_np(v.dtype), kind="ExternalInput").ap() for k, v in arrays.items()]
    args += [nc.dram_tensor(f"out_{i}", s, mybir.dt.from_np(np.dtype(d)), kind="ExternalOutput").ap()
             for i, (s, d) in enumerate(_OUTS)]
    two_layer_rgcn(nc, *args)
    r = run_bass_kernel_spmd(nc, [arrays], core_ids=[0])
    return r.results[0]["out_0"]
```

```python
from contextlib import ExitStack

import numpy as np

import concourse.bass as bass
from concourse import mybir

P = 128
D = 64
T = 4
RING = 4
A, B = 4, 4
WIN = 4
NG = 8
EPS = 1e-5

ALU = mybir.AluOpType
ACT = mybir.ActivationFunctionType
AX = mybir.AxisListType
F32 = mybir.dt.float32
BF16 = mybir.dt.bfloat16
I32 = mybir.dt.int32
I16 = mybir.dt.int16


def padded_tiles(n):
    return -(-n // (P * NG)) * NG


class Step:

    def __init__(self, turn, u, total, past=0):
        self.turn, self.u, self.total, self.past = turn + u // RING, u % RING, total, past
        self.fixed = isinstance(turn, int)

    def back(self, lag):
        return Step(self.turn, self.u - lag, self.total, self.past)

    @property
    def live(self):
        return not self.fixed or 0 <= RING * self.turn + self.u < self.total

    @property
    def n(self):
        return self.turn * RING + self.u

    def had(self, n):
        return not self.fixed or RING * self.turn + self.u >= n

    def count(self, each=1, ago=0):
        return (self.turn * RING + self.past * self.total + (self.u + 1 - ago)) * each

    def uses(self, each, ago=0):
        per_pass = (self.total - self.u + RING - 1) // RING
        return (self.turn + self.past * per_pass + (1 - ago)) * each


def pipeline(eng, total, lags, step, past=0, head=1):
    turns = total // RING - head
    for s in range(RING * head):
        step(Step(s // RING, s % RING, total, past))
    with eng.Fori(head, head + turns) as turn:
        for u in range(RING):
            step(Step(turn, u, total, past))
    for s in range(RING * (head + turns), total + lags):
        step(Step(s // RING, s % RING, total, past))


def two_layer_rgcn(nc, x, src_cols, dst_rows, dst_cols, type_rows, type_cols, W0, V1, comp1, bias1, loop1, out):
    N = x.shape[0]
    R = W0.shape[0]
    NB = V1.shape[0]
    NT = padded_tiles(N)
    NF = N // P
    NR = N - NF * P
    ET = dst_cols.shape[1]
    QUADS = ET // T
    GROUPS = NT // NG
    TPP = dst_rows.shape[1] // P
    EP = type_rows.shape[1]
    WC = WIN * D
    LAST = (NT - 1) * D
    assert R == A * B and A == 4 and ET % T == 0 and D * 2 == P
    assert QUADS * T == NT and NF // T == QUADS - 1 and NF % T and NR

    with ExitStack() as ctx:
        def sb(name, shape, dt=F32):
            return ctx.enter_context(nc.sbuf_tensor(name, shape, dt))

        def psum(name, shape):
            return ctx.enter_context(nc.psum_tensor(name, shape, F32))

        def sem(name):
            return ctx.enter_context(nc.semaphore(name))

        mask_dram = nc.dram_tensor("mask_dram", [A, ET * P], BF16).ap()
        span_dram = nc.dram_tensor("span_dram", [2, ET], I32).ap()
        x1_dram = nc.dram_tensor("x1_dram", [P, NT * D], F32).ap()
        h1_dram = nc.dram_tensor("h1_dram", [P * NT, D], F32).ap()

        acc = sb("acc", [P, (NT + WIN - 1) * D])
        iota = sb("iota", [P, WIN * P], I16)
        row_i = sb("row_i", [P, 1], I32)
        row = sb("row", [P, 1])
        ident = sb("ident", [P, P])
        eps = sb("eps", [P, 1])
        zero = sb("zero", [P, 1])
        src_i = sb("src_i", [P, ET], I32)
        src_h = sb("src_h", [P, ET], I32)
        dst_i = sb("dst_i", [P, ET], I32)
        low_i = sb("low_i", [P, ET], I32)
        low_f = sb("low_f", [P, ET])
        rel0 = sb("rel0", [P, ET])
        rel = sb("rel", [P, ET])
        drow = sb("drow", [ET // TPP, TPP, P], I32)
        lohi = sb("lohi", [ET // TPP, 2, TPP], I32)
        span = sb("span", [P, 2, ET], I32)
        wide = sb("wide", [P, ET], I32)
        widest = sb("widest", [P, 1], I32)
        passes = sb("passes", [P, 1], I32)
        off0 = sb("off0", [1, QUADS, T], I32)
        off = sb("off", [1, QUADS, T], I32)
        type_r = sb("type_r", [P, EP], I32)
        type_a = sb("type_a", [P, EP], I32)
        mask_r = sb("mask_r", [P, A, EP], BF16)
        type_c = sb("type_c", [P, ET], I32)
        type_b = sb("type_b", [P, ET], I32)
        is_b = sb("is_b", [P, ET, B])
        w0 = sb("w0", [P, 2, B, D])
        w1 = sb("w1", [P, 2 * B, D])
        wt = sb("wt", [P, 2 * B, D])
        v1 = sb("v1", [P, NB, D])
        comp = sb("comp", [P, 2 * B, NB])
        loopw = sb("loopw", [P, 2, D])
        bias = sb("bias", [P, D])
        idx = sb("idx", [P, RING, T], I32)
        mask = sb("mask", [P, RING, 2, T * P], BF16)
        rows = sb("rows", [P, RING, T, D])
        x_part = sb("x_part", [P, RING, T, D])
        first_pass = sb("first_pass", [P, 1])
        sums = sb("sums", [P, RING, NG])
        mean = sb("mean", [P, RING, NG])
        spread = sb("spread", [P, RING, NG])
        std = sb("std", [P, RING, NG])
        rstd = sb("rstd", [P, RING, NG])
        pick = sb("pick", [P, RING, T, B])
        total = sb("total", [P, 2, T])
        squares = sb("squares", [P, 2, T])
        twice = sb("twice", [P, 2, T, 2, D])
        masked = sb("masked", [P, 2, 2, T * P])
        picked = sb("picked", [P, 2, T, B, D])
        half = sb("half", [P, 2, T, 2, D])
        msg = sb("msg", [P, 2, T, D])
        rest = sb("rest", [P, 2, T, D])
        low = sb("low", [P, 2, T, D], BF16)
        hot = sb("hot", [P, 2, T, WIN * P], BF16)
        negm = sb("negm", [P, 2, T])
        iota_i = hot[:, 0, 0:2].rearrange("p t w -> p (t w)").bitcast(I32)
        dense = sb("dense", [P, RING, NG * D])
        square_of = dense[:, 0].rearrange("p (i t d) -> p i t d", i=2, t=T)
        square_of_x1 = half[:].rearrange("p i t b d -> p i (t b d)")
        shown = picked[:].rearrange("p i t b d -> p (i t b d)").rearrange("p (r n) -> p r n", r=RING)
        hT_sb = masked[:].rearrange("p i q e -> p (i q) e")

        ps_t = [psum(f"ps_t{i}", [P, T * P]) for i in range(2)]
        ps_y = [[psum(f"ps_y{i}{j}", [P, 2, B, D]) for j in range(2)] for i in range(2)]
        ps_w = [psum(f"ps_w{i}", [P, 2, WC]) for i in range(2)]

        const_in = sem("const_in")
        edges_in = sem("edges_in")
        src_in = sem("src_in")
        acc_zero = sem("acc_zero")
        zero_made = sem("zero_made")
        made = sem("made")
        c_dve = sem("c_dve")
        span_out = sem("span_out")
        span_in = sem("span_in")
        mask_out = sem("mask_out")
        ready = sem("ready")

        class Layer:

            def __init__(s, n):
                s.idx_in = [sem(f"idx_in{n}{i}") for i in range(RING)]
                s.mask_in = [sem(f"mask_in{n}{i}") for i in range(RING)]
                s.rows_in = [sem(f"rows_in{n}{i}") for i in range(RING)]
                s.total_done = sem(f"total_done{n}")
                s.squares_done = sem(f"squares_done{n}")
                s.std_done = sem(f"std_done{n}")
                s.rstd_done = sem(f"rstd_done{n}")
                s.pick_done = sem(f"pick_done{n}")
                s.twice_done = sem(f"twice_done{n}")
                s.turned = sem(f"turned{n}")
                s.masked_done = sem(f"masked_done{n}")
                s.prod_done = sem(f"prod_done{n}")
                s.picked_done = sem(f"picked_done{n}")
                s.negm_done = sem(f"negm_done{n}")
                s.half_done = sem(f"half_done{n}")
                s.other_half_done = sem(f"other_half_done{n}")
                s.hot_lag, s.sum_lag, s.won_lag = 2, 3, 4
                s.head = 2
                s.pick_lag = n + 1
                s.pool_tiles = (T, T // 2)[n]
                s.rest_done = sem(f"rest_done{n}")
                s.low_done = sem(f"low_done{n}")
                s.msg_done = sem(f"msg_done{n}")
                s.hot_done = sem(f"hot_done{n}")
                s.win_done = sem(f"win_done{n}")
                s.added = sem(f"added{n}")
                s.x_in = [sem(f"x_in{n}{i}") for i in range(RING)]
                s.x_tail = sem(f"x_tail{n}")
                s.x_added = sem(f"x_added{n}")
                s.start = sem(f"start{n}")
                s.moved = sem(f"moved{n}")

        layers = [Layer(0), Layer(1)]
        held = {name: sem(f"held_{name}") for name in ("pool", "sp", "dve")}

        x1_done = sem("x1_done")
        m_sum = sem("m_sum")
        m_mean = sem("m_mean")
        m_square = sem("m_square")
        m_spread = sem("m_spread")
        m_std = sem("m_std")
        m_rstd = sem("m_rstd")
        m_cent = sem("m_cent")
        m_h = sem("m_h")
        m_x1_out = [sem(f"m_x1_out{i}") for i in range(RING)]
        m_h_out = [sem(f"m_h_out{i}") for i in range(RING)]
        m_turned = sem("m_turned")
        m_hT = sem("m_hT")
        m_loop = sem("m_loop")
        m_acc = sem("m_acc")
        f_x1_in = [sem(f"f_x1_in{i}") for i in range(RING)]
        f_bias = sem("f_bias")
        f_sum = sem("f_sum")
        f_out = [sem(f"f_out{i}") for i in range(RING)]

        acc_tiles = acc[:].rearrange("p (t d) -> p t d", d=D)
        HALF_ACC = NT // 2 * D
        HT_LAG, ACC_LAG = 4, 6
        HALVES_AFTER = 5

        def dense_tiles(s):
            return dense[:, s.u].rearrange("p (t d) -> p t d", d=D)


        def loops(s):
            return ps_y[s.u % 2][0][:].rearrange("n j b o -> n (j b o)").rearrange("n (j m) -> n j m", m=2 * D)

        def load_passes(eng, kind):
            return nc.values_load(passes[0:1, 0:1], engines=[kind], min_val=1, max_val=-(-NT // WIN),
                                  skip_runtime_bounds_check_because="a span of node tiles over WIN")

        def high(words):
            return words.bitcast(BF16).rearrange("... (d two) -> ... d two", two=2)[..., 1]

        def group_dram(table, n):
            return table[bass.ds(n * (NG * P), NG * P), :].rearrange("(t p) d -> p t d", p=P)

        def pass_start(eng, L, k):
            eng.wait_ge(L.start, k + 1)

        block = ctx.enter_context(nc.Block())

        @block.sync
        def _(sp):
            sp.dma_start(drow[:], dst_rows.rearrange("q (t e) -> q t e", e=P)).then_inc(edges_in, 16)
            sp.dma_start(type_r[:], type_rows).then_inc(edges_in, 16)
            sp.dma_start(dst_i[:], dst_cols).then_inc(edges_in, 16)
            sp.dma_start(type_c[:], type_cols).then_inc(edges_in, 16)
            sp.dma_start(src_i[:], src_cols).then_inc(src_in, 16)
            sp.wait_ge(c_dve, 4)
            sp.dma_start(span_dram.rearrange("h (q t) -> q h t", t=TPP), lohi[:]).then_inc(span_out, 16)
            sp.wait_ge(span_out, 16)
            sp.dma_start(span[0:1], span_dram.unsqueeze(0)).then_inc(span_in, 16)
            sp.dma_start(low_i[:], span_dram[0].unsqueeze(0).broadcast_to([P, ET])).then_inc(span_in, 16)
            sp.wait_ge(c_dve, 9)
            sp.dma_start(mask_dram.rearrange("a (q e) -> q a e", e=EP), mask_r[:]).then_inc(mask_out, 16)
            sp.wait_ge(mask_out, 16)

            def x_load(L, s):
                if not s.fixed or s.n < NF // T:
                    sp.dma_start(x_part[:, s.u],
                                 x[bass.ds(s.n * (T * P), T * P), :].rearrange("(t p) d -> p t d", p=P)).then_inc(L.x_in[s.u], 16)
                else:
                    sp.dma_start(x_part[:, s.u, 0:NF % T],
                                 x[s.n * T * P:NF * P, :].rearrange("(t p) d -> p t d", p=P)).then_inc(L.x_in[s.u], 16)
                    sp.dma_start(x_part[0:NR, s.u, NF % T], x[NF * P:N, :]).then_inc(L.x_tail, 16)

            def edge_loads(L, layer, index):
                passes_r = load_passes(sp, mybir.EngineType.SP)

                def step(s):
                    if not s.live:
                        return
                    if s.had(RING):
                        sp.wait_ge(L.rows_in[s.u], s.uses(16 * T, ago=1))
                        sp.sem_inc(held["sp"], 1)
                    sp.dma_start(idx[:, s.u], index[:, bass.ds(s.n * T, T)]).then_inc(L.idx_in[s.u], 16)
                    if s.had(RING):
                        sp.wait_ge(L.masked_done, s.count(ago=RING))
                        sp.sem_inc(held["sp"], 1)
                    for p in range(2):
                        for a2 in range(2):
                            sp.dma_start(
                                mask[a2 * D:a2 * D + D, s.u, p],
                                mask_dram[2 * p + a2, bass.ds(s.n * (T * P), T * P)].unsqueeze(0)
                                .broadcast_to([D, T * P])).then_inc(L.mask_in[s.u], 16)
                    if layer == 0:
                        if s.had(RING):
                            sp.wait_ge(L.x_added, s.count(ago=RING))
                            sp.sem_inc(held["sp"], 1)
                        x_load(L, s)

                with sp.Fori(0, passes_r) as k:
                    pass_start(sp, L, k)
                    pipeline(sp, QUADS, 0, step, k)

            sp.wait_ge(ready, 1)
            sp.wait_ge(src_in, 16)
            edge_loads(layers[0], 0, src_i)

            def mid(s):
                b = s.back(3)
                if b.live:
                    if b.fixed and b.n == 0:
                        sp.wait_ge(x1_done, 1)
                    columns = bass.ds(b.n * (NG * D), NG * D)
                    if b.had(RING):
                        sp.wait_ge(m_acc, b.count(ago=RING))
                        sp.sem_inc(held["sp"], 1)
                    sp.dma_start(x1_dram[:, columns], acc[:, columns]).then_inc(m_x1_out[b.u], 16)
                    sp.wait_ge(m_h, b.count())
                    sp.sem_inc(held["sp"], 1)
                    sp.dma_start(h1_columns[:, columns], shown[:, b.u]).then_inc(m_h_out[b.u], 16)

            h1_columns = h1_dram.rearrange("(p t) d -> p (t d)", p=P)
            pipeline(sp, GROUPS, 3, mid, head=2)
            sp.wait_ge(ready, 2)
            edge_loads(layers[1], 1, src_h)
            for u in range(RING):
                sp.wait_ge(m_x1_out[u], 16 * ((GROUPS - u + RING - 1) // RING))
                sp.wait_ge(m_h_out[u], 16 * ((GROUPS - u + RING - 1) // RING))

            def last(s):
                if s.live:
                    if s.had(RING):
                        sp.wait_ge(f_out[s.u], s.uses(16, ago=1))
                        sp.sem_inc(held["sp"], 1)
                    sp.dma_start(dense[:, s.u], x1_dram[:, bass.ds(s.n * (NG * D), NG * D)]).then_inc(f_x1_in[s.u], 16)
                w = s.back(2)
                if w.live:
                    sp.wait_ge(f_sum, w.count())
                    sp.sem_inc(held["sp"], 1)
                    whole = not w.fixed or (w.n + 1) * NG <= NF
                    shown = dense[:, w.u].rearrange("p (t d) -> p t d", d=D)
                    if whole:
                        sp.dma_start(group_dram(out, w.n), shown).then_inc(f_out[w.u], 16)
                    else:
                        t0 = NF - w.n * NG
                        if t0:
                            sp.dma_start(out[w.n * NG * P:NF * P, :].rearrange("(t p) d -> p t d", p=P),
                                         shown[:, 0:t0]).then_inc(f_out[w.u], 16)
                        if NR:
                            sp.dma_start(out[NF * P:N, :], shown[0:NR, t0]).then_inc(f_out[w.u], 16)

            pipeline(sp, GROUPS, 2, last)
            ends = [16 * ((GROUPS - u + RING - 1) // RING) for u in range(RING)]
            ends[(GROUPS - 1) % RING] += 16 * ((NF > (GROUPS - 1) * NG) + (NR > 0) - 1)
            for u in range(RING):
                sp.wait_ge(f_out[u], ends[u])

        @block.gpsimd
        def _(pool):
            nc.gpsimd.memset(loopw[:], 0.0).then_inc(made, 1)
            nc.gpsimd.memset(zero[:], 0.0).then_inc(zero_made, 1)
            nc.gpsimd.iota(iota_i, pattern=[[1, WIN * P]], base=0, channel_multiplier=0).then_inc(made, 1)
            nc.gpsimd.iota(row_i[:], pattern=[[0, 1]], base=0, channel_multiplier=1).then_inc(made, 1)
            nc.gpsimd.memset(eps[:], EPS).then_inc(made, 1)
            nc.gpsimd.memset(first_pass[:], 1.0).then_inc(made, 1)
            nc.gpsimd.memset(acc[:, 0:HALF_ACC], 0.0).then_inc(acc_zero, 1)
            def gathers(L, layer, table):
                passes_r = load_passes(pool, mybir.EngineType.Pool)

                def halve(s):
                    i, n = s.u % 2, L.pool_tiles
                    pool.wait_ge(L.picked_done, s.count(each=2) - (T - n) // 2)
                    if s.had(2):
                        pool.wait_ge(L.msg_done, s.count(ago=2))
                    nc.gpsimd.tensor_tensor(half[:, i, 0:n], picked[:, i, 0:n, 0:2], picked[:, i, 0:n, 2:4],
                                            ALU.add).then_inc(L.half_done, 1)

                def step(s):
                    if s.back(HALVES_AFTER).live:
                        halve(s.back(HALVES_AFTER))
                    if s.live:
                        gather(s)

                def gather(s):
                    pool.wait_ge(L.idx_in[s.u], s.uses(16))
                    if s.had(RING):
                        pool.wait_ge(L.squares_done if layer == 0 else L.twice_done, s.count(ago=RING))
                    pool.sem_inc(held["pool"], 1)
                    for t in range(T):
                        nc.gpsimd.indirect_dma_start(
                            out=rows[:, s.u, t], out_offset=None, in_=table,
                            in_offset=bass.IndirectOffsetOnAxis(ap=idx[:, s.u, t:t + 1], axis=0),
                        ).then_inc(L.rows_in[s.u], 16)

                with pool.Fori(0, passes_r) as k:
                    pass_start(pool, L, k)
                    pipeline(pool, QUADS, HALVES_AFTER, step, k, head=2)

            pool.wait_ge(ready, 1)
            gathers(layers[0], 0, x)

            def mid(s):
                if s.had(RING):
                    pool.wait_ge(m_h, s.count(ago=RING))
                pool.wait_ge(m_mean, s.count())
                nc.gpsimd.tensor_tensor(dense_tiles(s), acc_tiles[:, bass.ds(s.n * NG, NG)],
                                        mean[:, s.u].unsqueeze(2).broadcast_to([P, NG, D]),
                                        ALU.subtract).then_inc(m_cent, 1)

            pipeline(pool, GROUPS, 0, mid)
            for u in range(RING):
                pool.wait_ge(m_h_out[u], 16 * ((GROUPS - u + RING - 1) // RING))
            gathers(layers[1], 1, h1_dram)

        @block.tensor
        def _(pe):
            def edge_products(L, weights, layer):
                passes_r = load_passes(pe, mybir.EngineType.PE)

                def turn_rows(s):
                    pe.wait_ge(L.twice_done, s.count())
                    if s.had(2):
                        pe.wait_ge(L.masked_done, s.count(ago=2))
                    for t in range(T):
                        mm = pe.transpose(ps_t[s.u % 2][:, t * P:t * P + P],
                                          twice[:, s.u % 2, t].rearrange("e a d -> e (a d)"), ident[:])
                    mm.then_inc(L.turned, 1)

                def products(s):
                    pe.wait_ge(L.masked_done, s.count())
                    for h in range(2):
                        if s.had(2):
                            pe.wait_ge(L.picked_done, s.count(each=2, ago=2) - (1 - h))
                        for j in range(2):
                            t = 2 * h + j
                            for p in range(2):
                                mm = pe.matmul(ps_y[s.u % 2][h][:, j].rearrange("e b o -> e (b o)"),
                                               masked[:, s.u % 2, p, t * P:t * P + P],
                                               weights(p), start=(p == 0), stop=(p == 1))
                        mm.then_inc(L.prod_done, 1)

                def windows(s):
                    pe.wait_ge(L.hot_done, s.count())
                    pe.wait_ge(L.low_done, s.count())
                    for h in range(2):
                        if s.had(1):
                            pe.wait_ge(L.added, s.count(each=T, ago=1) - (2 - 2 * h))
                        for j in range(2):
                            t = 2 * h + j
                            parts = high(msg[:, s.u % 2, t]), high(rest[:, s.u % 2, t]), low[:, s.u % 2, t]
                            for w in range(WIN):
                                for n, part in enumerate(parts):
                                    mm = pe.matmul(ps_w[h][:, j, w * D:w * D + D],
                                                   hot[:, s.u % 2, t, w * P:w * P + P],
                                                   part, start=(n == 0), stop=(n == 2))
                        mm.then_inc(L.win_done, 1)

                def step(s):
                    if layer == 1 and s.live:
                        turn_rows(s)
                    if s.back(1).live:
                        products(s.back(1))
                    if layer == 0 and s.live:
                        turn_rows(s)
                    if s.back(L.sum_lag).live:
                        windows(s.back(L.sum_lag))

                with pe.Fori(0, passes_r) as k:
                    pass_start(pe, L, k)
                    pipeline(pe, QUADS, L.won_lag, step, k, head=L.head)

            pe.wait_ge(ready, 1)
            pe.wait_ge(const_in, 16 * 13)
            edge_products(layers[0], lambda p: w0[:, p].rearrange("k b o -> k (b o)"), 0)

            def mid(s):
                t = s.back(3)
                if t.live:
                    pe.wait_ge(m_h, t.count())
                    if t.had(2):
                        pe.wait_ge(m_hT, t.count(ago=2))
                    for j in range(NG // 2):
                        mm = pe.transpose(ps_t[t.u % 2][:, j * P:j * P + P], shown[:, t.u, j * P:j * P + P], ident[:])
                    mm.then_inc(m_turned, 1)
                b = s.back(4)
                if b.live:
                    pe.wait_ge(m_hT, b.count())
                    if b.had(2):
                        pe.wait_ge(m_acc, b.count(ago=2))
                    for j in range(NG // 2):
                        mm = pe.matmul(loops(b)[:, j], hT_sb[:, b.u, j * P:j * P + P],
                                       loopw[:].rearrange("k a o -> k (a o)"), start=True, stop=True)
                    mm.then_inc(m_loop, 1)

            pipeline(pe, GROUPS, 4, mid, head=2)
            pe.wait_ge(ready, 3)
            edge_products(layers[1], lambda p: w1[:, p * B:p * B + B].rearrange("k b o -> k (b o)"), 1)

        @block.scalar
        def _(act):
            def edge_picks(L, layer):
                passes_r = load_passes(act, mybir.EngineType.Activation)

                def square(s):
                    if s.had(2):
                        act.wait_ge(L.rstd_done, s.count(ago=2))
                    for t in range(T):
                        a = act.activation(square_of[:, s.u % 2, t], rows[:, s.u, t], ACT.Square, bias=negm[:, s.u % 2, t:t + 1],
                                           accum_out=squares[:, s.u % 2, t:t + 1])
                    a.then_inc(L.squares_done, 1)

                def deviation(s):
                    act.wait_ge(L.squares_done, s.count())
                    act.activation(std[:, s.u % 2, 0:T], squares[:, s.u % 2], ACT.Sqrt,
                                   scale=1.0 / D, bias=eps[:]).then_inc(L.std_done, 1)

                def picks(s):
                    if layer == 0:
                        act.wait_ge(L.pick_done, s.count())
                    if s.had(2):
                        act.wait_ge(L.half_done, s.count(ago=2))
                        if L.pool_tiles < T:
                            act.wait_ge(L.other_half_done, s.count(ago=2))
                    for h in range(2):
                        act.wait_ge(L.prod_done, s.count(each=2) - (1 - h))
                        for j in range(2):
                            t = 2 * h + j
                            for b in range(B):
                                by = (pick[:, s.u, t, b:b + 1] if layer == 0 else
                                      is_b[:, bass.ds(s.n * T + t, 1), b])
                                a = act.activation(picked[:, s.u % 2, t, b], ps_y[s.u % 2][h][:, j, b],
                                                   ACT.Copy, scale=by)
                        a.then_inc(L.picked_done, 1)

                def double(s):
                    act.wait_ge(L.rows_in[s.u], s.uses(16 * T))
                    if s.had(2):
                        act.wait_ge(L.turned, s.count(ago=2))
                    act.activation(twice[:, s.u % 2], rows[:, s.u].unsqueeze(2).broadcast_to([P, T, 2, D]),
                                   ACT.Copy).then_inc(L.twice_done, 1)

                def centre(s):
                    act.wait_ge(L.negm_done, s.count())
                    if s.had(2):
                        act.wait_ge(L.turned, s.count(ago=2))
                    for t in range(T):
                        a = act.activation(twice[:, s.u % 2, t],
                                           rows[:, s.u, t].unsqueeze(1).broadcast_to([P, 2, D]),
                                           ACT.Relu, bias=negm[:, s.u % 2, t:t + 1])
                    a.then_inc(L.twice_done, 1)

                def step(s):
                    if s.live:
                        if layer == 0:
                            centre(s)
                            square(s)
                            deviation(s)
                        else:
                            double(s)
                    if s.back(L.pick_lag).live:
                        picks(s.back(L.pick_lag))

                with act.Fori(0, passes_r) as k:
                    pass_start(act, L, k)
                    pipeline(act, QUADS, L.won_lag, step, k, head=L.head)

            act.wait_ge(zero_made, 1)
            rest_acc = acc[:, HALF_ACC:]
            act.activation(rest_acc, zero[:, 0:1].broadcast_to([P, rest_acc.shape[1]]), ACT.Copy).then_inc(acc_zero, 1)
            w_split = W0.rearrange("(p a b) d o -> a d p b o", p=2, a=2)
            v_split = V1.rearrange("c d o -> d c o")
            comp_split = comp1.rearrange("(p a b) c -> a p b c", p=2, a=2)
            act.wait_ge(made, 5)
            for a2 in range(2):
                half_p = slice(a2 * D, a2 * D + D)
                for p in range(2):
                    act.dma_start(w0[half_p, p], w_split[a2, :, p]).then_inc(const_in, 16)
                    act.dma_start(comp[half_p, p * B:p * B + B],
                                 comp_split[a2, p].unsqueeze(0).broadcast_to([D, B, NB])).then_inc(const_in, 16)
                act.dma_start(v1[half_p], v_split).then_inc(const_in, 16)
                act.dma_start(loopw[half_p, a2], loop1).then_inc(const_in, 16)
            act.dma_start(bias[:], bias1.unsqueeze(0).broadcast_to([P, D])).then_inc(const_in, 16)
            act.wait_ge(ready, 1)
            edge_picks(layers[0], 0)

            def mid(s):
                q = s.back(1)
                if q.live:
                    act.wait_ge(m_cent, q.count())
                    if q.had(2):
                        act.wait_ge(m_spread, q.count(ago=2))
                    act.activation(square_of_x1[:, q.u % 2], dense[:, q.u], ACT.Square).then_inc(m_square, 1)
                c = s.back(HT_LAG)
                if c.live:
                    if c.had(RING):
                        act.wait_ge(m_loop, c.count(ago=RING))
                    act.wait_ge(m_turned, c.count())
                    act.activation(hT_sb[:, c.u], ps_t[c.u % 2][:], ACT.Copy).then_inc(m_hT, 1)
                e = s.back(ACC_LAG)
                if e.live:
                    act.wait_ge(m_loop, e.count())
                    act.wait_ge(m_x1_out[e.u], e.uses(16))
                    act.activation(acc[:, bass.ds(e.n * (NG * D), NG * D)],
                                   loops(e).rearrange("n j m -> n (j m)"), ACT.Copy).then_inc(m_acc, 1)
                b = s.back(2)
                if b.live:
                    act.wait_ge(m_spread, b.count())
                    if b.had(RING):
                        act.wait_ge(m_rstd, b.count(ago=RING))
                    act.activation(std[:, b.u], spread[:, b.u], ACT.Sqrt, scale=1.0 / D, bias=eps[:]).then_inc(m_std, 1)

            pipeline(act, GROUPS, ACC_LAG, mid, head=3)
            edge_picks(layers[1], 1)

        @block.vector
        def _(dve):
            steps = [0]

            def done(ins):
                steps[0] += 1
                ins.then_inc(c_dve, 1)
                dve.wait_ge(c_dve, steps[0])

            dve.wait_ge(edges_in, 16 * 4)
            dve.wait_ge(src_in, 16)
            done(dve.tensor_reduce(lohi[:, 0], drow[:], AX.X, ALU.min))
            done(dve.tensor_scalar(lohi[:, 0], lohi[:, 0], P.bit_length() - 1, None, ALU.arith_shift_right))
            done(dve.tensor_reduce(lohi[:, 1], drow[:], AX.X, ALU.max))
            done(dve.tensor_scalar(lohi[:, 1], lohi[:, 1], P.bit_length() - 1, None, ALU.arith_shift_right))
            done(dve.tensor_scalar(type_a[:], type_r[:], B.bit_length() - 1, None, ALU.arith_shift_right))
            for a in range(A):
                done(dve.tensor_scalar(mask_r[:, a], type_a[:], float(a), None, ALU.is_equal))
            done(dve.tensor_scalar(type_b[:], type_c[:], B - 1, None, ALU.bitwise_and))
            for b in range(B):
                done(dve.tensor_scalar(is_b[:, :, b], type_b[:], float(b), None, ALU.is_equal))
            dve.wait_ge(made, 5)
            done(dve.tensor_copy(iota[:], iota_i))
            done(dve.tensor_copy(row[:], row_i[:]))
            done(dve.tensor_scalar(ident[:], iota[:, 0:P], row[:, 0:1], None, ALU.is_equal))
            dve.wait_ge(span_in, 32)
            done(dve.tensor_tensor(wide[0:1], span[0:1, 1], span[0:1, 0], ALU.subtract))
            done(dve.tensor_reduce(widest[0:1], wide[0:1], AX.X, ALU.max))
            done(dve.tensor_scalar(widest[0:1], widest[0:1], WIN.bit_length() - 1, None, ALU.arith_shift_right))
            done(dve.tensor_scalar(passes[0:1], widest[0:1], 1, None, ALU.add))
            dve.nop().then_inc(layers[0].start, 1)
            dve.nop().then_inc(ready, 1)

            def edge_sums(L, layer):
                passes_r = load_passes(dve, mybir.EngineType.DVE)

                def sum_rows(s):
                    dve.wait_ge(L.rows_in[s.u], s.uses(16 * T))
                    dve.tensor_reduce(total[:, s.u % 2], rows[:, s.u], AX.X, ALU.add).then_inc(L.total_done, 1)

                def negate(s):
                    i = s.u % 2
                    dve.wait_ge(L.total_done, s.count())
                    if s.had(2):
                        dve.wait_ge(L.squares_done, s.count(ago=2))
                    dve.tensor_scalar(negm[:, i], total[:, i], -1.0 / D, None, ALU.mult).then_inc(L.negm_done, 1)

                def invert(s):
                    i = s.u % 2
                    dve.wait_ge(L.std_done, s.count())
                    dve.reciprocal(rstd[:, i, 0:T], std[:, i, 0:T]).then_inc(L.rstd_done, 1)

                def deviate(s):
                    i = s.u % 2
                    dve.wait_ge(L.rstd_done, s.count())
                    if s.had(RING):
                        dve.wait_ge(L.picked_done, s.count(each=2, ago=RING))
                    dve.tensor_tensor(pick[:, s.u], is_b[:, bass.ds(s.n * T, T)],
                                      rstd[:, i, 0:T].unsqueeze(2).broadcast_to([P, T, B]),
                                      ALU.mult).then_inc(L.pick_done, 1)

                def mask_rows(s):
                    i = s.u % 2
                    dve.wait_ge(L.turned, s.count())
                    dve.wait_ge(L.mask_in[s.u], s.uses(16 * 4))
                    if s.had(2):
                        dve.wait_ge(L.prod_done, s.count(each=2, ago=2))
                    for p in range(2):
                        m = dve.tensor_tensor(masked[:, i, p], ps_t[i][:], mask[:, s.u, p], ALU.mult)
                    m.then_inc(L.masked_done, 1)

                def one_hot(s, t):
                    i = s.u % 2
                    if t == 0:
                        if s.had(2):
                            dve.wait_ge(L.win_done, s.count(each=2, ago=2))
                    h = dve.tensor_scalar(hot[:, i, t], iota[:], rel[:, bass.ds(s.n * T + t, 1)], None,
                                          ALU.is_equal)
                    if t == T - 1:
                        h.then_inc(L.hot_done, 1)

                def halve(s):
                    i, n = s.u % 2, L.pool_tiles
                    dve.wait_ge(L.picked_done, s.count(each=2))
                    if s.had(2):
                        dve.wait_ge(L.msg_done, s.count(ago=2))
                    dve.tensor_tensor(half[:, i, n:T], picked[:, i, n:T, 0:2], picked[:, i, n:T, 2:4],
                                      ALU.add).then_inc(L.other_half_done, 1)

                def sum_up(s):
                    i = s.u % 2
                    dve.wait_ge(L.half_done, s.count())
                    if L.pool_tiles < T:
                        dve.wait_ge(L.other_half_done, s.count())
                    if s.had(2):
                        dve.wait_ge(L.win_done, s.count(each=2, ago=2))
                    dve.tensor_tensor(msg[:, i], half[:, i, :, 0], half[:, i, :, 1], ALU.add).then_inc(L.msg_done, 1)

                def split_rest(s):
                    i = s.u % 2
                    dve.wait_ge(L.msg_done, s.count())
                    dve.tensor_tensor(rest[:, i], msg[:, i], high(msg[:, i]), ALU.subtract).then_inc(L.rest_done, 1)

                def split_low(s):
                    i = s.u % 2
                    dve.wait_ge(L.rest_done, s.count())
                    dve.tensor_tensor(low[:, i], rest[:, i], high(rest[:, i]), ALU.subtract).then_inc(L.low_done, 1)

                def add_x(s):
                    dve.wait_ge(L.x_in[s.u], s.uses(16))
                    if s.fixed and s.n == NF // T:
                        dve.wait_ge(L.x_tail, (s.past + 1) * 16)
                    if s.back(L.won_lag).live:
                        dve.wait_ge(L.added, s.back(L.won_lag).count(each=T))
                    if s.had(1):
                        dve.wait_ge(L.x_added, s.count(ago=1))
                    to = acc[:, bass.ds(s.n * (T * D), T * D)]
                    dve.scalar_tensor_tensor(to, x_part[:, s.u].rearrange("p t d -> p (t d)"), first_pass[:, 0:1],
                                             to, ALU.mult, ALU.add).then_inc(L.x_added, 1)

                def add_window(s, t, at):
                    if t % 2 == 0:
                        dve.wait_ge(L.win_done, s.count(each=2) - (1 - t // 2))
                    before = s.back(1 - L.won_lag)
                    if layer == 0 and t == 0 and before.live:
                        dve.wait_ge(L.x_added, before.count())
                    if s.had(1) or t > 0:
                        dve.wait_ge(L.added, s.count(each=T) - (T - t))
                    to = acc[:, bass.ds(at, WC)]
                    dve.tensor_tensor(to, ps_w[t // 2][:, t % 2], to, ALU.add).then_inc(L.added, 1)

                def step(s):
                    new, turned, marked, summed, won = (s.back(lag) for lag in (0, 1, L.hot_lag, L.sum_lag, L.won_lag))
                    ln, lt = layer == 0 and new.live, layer == 0 and turned.live
                    if won.live:
                        at = nc.values_load_multi_w_load_instructions(
                            off[:, bass.ds(won.n, 1)].rearrange("p q t -> p (q t)"), engines=[mybir.EngineType.DVE],
                            min_val=0, max_val=LAST,
                            skip_runtime_bounds_check_because="the windows are held to acc where they are set")[1]

                    def tile(t):
                        if won.live:
                            add_window(won, t, at[t])
                        if marked.live:
                            one_hot(marked, t)

                    if ln:
                        sum_rows(new)
                    if turned.live:
                        mask_rows(turned)
                    if ln:
                        negate(new)
                    tile(0)
                    if summed.live:
                        sum_up(summed)
                    tile(1)
                    if summed.live:
                        split_rest(summed)
                    if lt:
                        invert(turned)
                    tile(2)
                    if lt:
                        deviate(turned)
                    if summed.live:
                        split_low(summed)
                    tile(3)
                    if ln:
                        add_x(new)
                    if marked.live and L.pool_tiles < T:
                        halve(marked)

                with dve.Fori(0, passes_r) as k:
                    pipeline(dve, QUADS, L.won_lag, step, k, head=L.head)
                    dve.wait_ge(L.added, (k + 1) * (QUADS * T))
                    if layer == 0:
                        dve.wait_ge(L.x_added, (k + 1) * QUADS)
                        dve.memset(first_pass[:], 0.0).then_inc(L.moved, 1)
                    dve.tensor_scalar(rel[:], rel[:], float(-WIN * P), None, ALU.add).then_inc(L.moved, 1)
                    dve.tensor_scalar(off[:], off[:], WC, LAST, ALU.add, ALU.min).then_inc(L.moved, 1)
                    dve.wait_ge(L.moved, (k + 1) * (3 if layer == 0 else 2))
                    dve.nop().then_inc(L.start, 1)

            done(dve.tensor_copy(low_f[:], low_i[:]))
            done(dve.tensor_copy(rel[:], dst_i[:]))
            done(dve.scalar_tensor_tensor(rel0[:], low_f[:], float(-P), rel[:], ALU.mult, ALU.add))
            by_quad = span[0:1, 0].rearrange("p (q t) -> p q t", t=T)
            done(dve.tensor_scalar(off0[:], by_quad, D, None, ALU.mult))
            done(dve.tensor_copy(rel[:], rel0[:]))
            done(dve.tensor_copy(off[:], off0[:]))
            done(dve.tensor_scalar(wide[:], src_i[:], P - 1, None, ALU.bitwise_and))
            done(dve.tensor_scalar(wide[:], wide[:], NT, None, ALU.mult))
            done(dve.tensor_scalar(src_h[:], src_i[:], P.bit_length() - 1, None, ALU.arith_shift_right))
            done(dve.tensor_tensor(src_h[:], src_h[:], wide[:], ALU.add))
            dve.nop().then_inc(ready, 1)
            dve.wait_ge(acc_zero, 2)
            edge_sums(layers[0], 0)
            dve.nop().then_inc(x1_done, 1)

            def mid(s):
                m, q, h = s.back(1), s.back(3), s.back(4)
                if m.live:
                    dve.wait_ge(m_sum, m.count())
                    if m.had(RING):
                        dve.wait_ge(m_cent, m.count(ago=RING))
                    dve.tensor_scalar(mean[:, m.u], sums[:, m.u], 1.0 / D, None, ALU.mult).then_inc(m_mean, 1)
                if s.live:
                    if s.had(RING):
                        dve.wait_ge(m_mean, s.count(ago=RING))
                    dve.tensor_reduce(sums[:, s.u], acc_tiles[:, bass.ds(s.n * NG, NG)], AX.X, ALU.add).then_inc(m_sum, 1)
                if h.live:
                    dve.wait_ge(m_std, h.count())
                    if h.had(RING):
                        dve.wait_ge(m_h, h.count(ago=RING))
                    dve.reciprocal(rstd[:, h.u], std[:, h.u]).then_inc(m_rstd, 1)
                    dve.wait_ge(m_rstd, h.count())
                    if h.had(RING):
                        dve.wait_ge(m_h_out[h.u], h.uses(16, ago=1))
                        dve.wait_ge(m_turned, h.count(ago=RING))
                    dve.scalar_tensor_tensor(shown[:, h.u].rearrange("p (t d) -> p t d", d=D), dense_tiles(h), 0.0,
                                             rstd[:, h.u].unsqueeze(2).broadcast_to([P, NG, D]),
                                             ALU.max, ALU.mult).then_inc(m_h, 1)
                if q.live:
                    dve.wait_ge(m_square, q.count())
                    if q.had(RING):
                        dve.wait_ge(m_std, q.count(ago=RING))
                    dve.tensor_reduce(spread[:, q.u], square_of_x1[:, q.u % 2].rearrange("p (t d) -> p t d", d=D),
                                      AX.X, ALU.add).then_inc(m_spread, 1)

            pipeline(dve, GROUPS, 4, mid, head=2)
            done(dve.tensor_copy(rel[:], rel0[:]))
            done(dve.tensor_copy(off[:], off0[:]))
            dve.nop().then_inc(layers[1].start, 1)
            dve.wait_ge(const_in, 16 * 13)
            for c in range(NB):
                to = w1 if c == 0 else wt
                done(dve.tensor_tensor(to[:], v1[:, c].unsqueeze(1).broadcast_to([P, 2 * B, D]),
                                       comp[:, :, c:c + 1].broadcast_to([P, 2 * B, D]), ALU.mult))
                if c:
                    done(dve.tensor_tensor(w1[:], w1[:], wt[:], ALU.add))
            dve.nop().then_inc(ready, 1)
            dve.wait_ge(m_acc, GROUPS)
            edge_sums(layers[1], 1)

            def last(s):
                if s.live:
                    part = acc_tiles[:, bass.ds(s.n * NG, NG)]
                    dve.tensor_tensor(part, part, bias[:].unsqueeze(1).broadcast_to([P, NG, D]),
                                      ALU.add).then_inc(f_bias, 1)
                b = s.back(1)
                if b.live:
                    dve.wait_ge(f_bias, b.count())
                    dve.wait_ge(f_x1_in[b.u], b.uses(16))
                    shown = dense[:, b.u]
                    dve.scalar_tensor_tensor(shown, acc[:, bass.ds(b.n * (NG * D), NG * D)], 0.0, shown,
                                             ALU.max, ALU.add).then_inc(f_sum, 1)

            pipeline(dve, GROUPS, 1, last)


_OUTS = [((50000, 64), "float32")]


def kernel(x, src, dst, edge_type_16, L0_gnn_weight, L1_gnn_weight, L1_gnn_w_comp, L1_gnn_h_bias, L1_gnn_loop_weight):
    import concourse.bacc as bacc
    from concourse.bass_utils import run_bass_kernel_spmd

    x = np.asarray(x)
    src, dst, kind = (np.asarray(v).astype(np.int32) for v in (src, dst, edge_type_16))
    n, e, rels = x.shape[0], src.shape[0], np.asarray(L0_gnn_weight).shape[0]
    tiles = padded_tiles(e)
    filled = [np.concatenate([v, np.full(tiles * P - e, c, np.int32)])
              for v, c in ((src, 0), (dst, n - 1), (kind, rels))]
    cols = [np.ascontiguousarray(v.reshape(tiles, P).T) for v in filled]
    arrays = {
        "x": x, "src_cols": cols[0], "dst_rows": filled[1].reshape(-1, T * P), "dst_cols": cols[1],
        "type_rows": filled[2].reshape(P, -1), "type_cols": cols[2],
        "W0": L0_gnn_weight, "V1": L1_gnn_weight, "comp1": L1_gnn_w_comp, "bias1": L1_gnn_h_bias,
        "loop1": L1_gnn_loop_weight,
    }
    arrays = {f"in_{k}": np.ascontiguousarray(v) for k, v in arrays.items()}
    nc = bacc.Bacc("TRN2", target_bir_lowering=False, num_devices=1)
    args = [nc.dram_tensor(k, v.shape, mybir.dt.from_np(v.dtype), kind="ExternalInput").ap() for k, v in arrays.items()]
    args += [nc.dram_tensor(f"out_{i}", s, mybir.dt.from_np(np.dtype(d)), kind="ExternalOutput").ap()
             for i, (s, d) in enumerate(_OUTS)]
    two_layer_rgcn(nc, *args)
    r = run_bass_kernel_spmd(nc, [arrays], core_ids=[0])
    return r.results[0]["out_0"]
```
